# Optimizing a Trainium2 kernel written in Bass

```python
import numpy as np
import jax
import jax.numpy as jnp

def _softmax(x, axis=-1):
    return jax.nn.softmax(x, axis=axis)

def _gelu(x):
    return jax.nn.gelu(x, approximate=True)

def _silu(x):
    return jax.nn.silu(x)

def _sigmoid(x):
    return jax.nn.sigmoid(x)

def _layernorm(x, axis=-1, eps=1e-05):
    m = jnp.mean(x, axis=axis, keepdims=True)
    v = jnp.var(x, axis=axis, keepdims=True)
    return (x - m) / jnp.sqrt(v + eps)

def _scatter_add(tgt, idx, src, axis=0):
    return tgt.at[idx].add(src)

def _segment_sum(src, seg, n):
    return jax.ops.segment_sum(src, seg, n)
kernel_name = 'mk_dlrm_tower_d1_rec_r8_c60da3'

def setup_inputs(seed: int=0):
    np.random.seed(seed)
    _w = jnp.asarray

    def _rec_inputs():
        import jax
        import jax.numpy as jnp
        _tk = jax.random.key(seed)
        dense_ctx = jax.random.normal(jax.random.fold_in(_tk, 190), (512, 16), jnp.float32)
        ids = jnp.stack([jax.random.randint(jax.random.fold_in(_tk, 200 + f), (512,), 0, v, jnp.int32) for f, v in enumerate([125000, 1250, 1250, 1000, 125000, 12500, 12500, 1000, 1250, 1250, 1250, 125000, 1250, 125000, 12500, 1250, 1250, 12500, 12500, 1250, 125000, 1250, 125000, 12500, 1250, 1000, 1250, 1000, 1000, 125000, 1000, 12500, 12500, 1250, 1250, 1250, 12500, 12500, 12500])], axis=1)
        tbl_0 = 0.05 * jax.random.normal(jax.random.fold_in(_tk, 500 + 0), (125000, 16), jnp.float32)
        tbl_1 = 0.05 * jax.random.normal(jax.random.fold_in(_tk, 500 + 1), (1250, 16), jnp.float32)
        tbl_2 = 0.05 * jax.random.normal(jax.random.fold_in(_tk, 500 + 2), (1250, 16), jnp.float32)
        tbl_3 = 0.05 * jax.random.normal(jax.random.fold_in(_tk, 500 + 3), (1000, 16), jnp.float32)
        tbl_4 = 0.05 * jax.random.normal(jax.random.fold_in(_tk, 500 + 4), (125000, 16), jnp.float32)
        tbl_5 = 0.05 * jax.random.normal(jax.random.fold_in(_tk, 500 + 5), (12500, 16), jnp.float32)
        tbl_6 = 0.05 * jax.random.normal(jax.random.fold_in(_tk, 500 + 6), (12500, 16), jnp.float32)
        tbl_7 = 0.05 * jax.random.normal(jax.random.fold_in(_tk, 500 + 7), (1000, 16), jnp.float32)
        tbl_8 = 0.05 * jax.random.normal(jax.random.fold_in(_tk, 500 + 8), (1250, 16), jnp.float32)
        tbl_9 = 0.05 * jax.random.normal(jax.random.fold_in(_tk, 500 + 9), (1250, 16), jnp.float32)
        tbl_10 = 0.05 * jax.random.normal(jax.random.fold_in(_tk, 500 + 10), (1250, 16), jnp.float32)
        tbl_11 = 0.05 * jax.random.normal(jax.random.fold_in(_tk, 500 + 11), (125000, 16), jnp.float32)
        tbl_12 = 0.05 * jax.random.normal(jax.random.fold_in(_tk, 500 + 12), (1250, 16), jnp.float32)
        tbl_13 = 0.05 * jax.random.normal(jax.random.fold_in(_tk, 500 + 13), (125000, 16), jnp.float32)
        tbl_14 = 0.05 * jax.random.normal(jax.random.fold_in(_tk, 500 + 14), (12500, 16), jnp.float32)
        tbl_15 = 0.05 * jax.random.normal(jax.random.fold_in(_tk, 500 + 15), (1250, 16), jnp.float32)
        tbl_16 = 0.05 * jax.random.normal(jax.random.fold_in(_tk, 500 + 16), (1250, 16), jnp.float32)
        tbl_17 = 0.05 * jax.random.normal(jax.random.fold_in(_tk, 500 + 17), (12500, 16), jnp.float32)
        tbl_18 = 0.05 * jax.random.normal(jax.random.fold_in(_tk, 500 + 18), (12500, 16), jnp.float32)
        tbl_19 = 0.05 * jax.random.normal(jax.random.fold_in(_tk, 500 + 19), (1250, 16), jnp.float32)
        tbl_20 = 0.05 * jax.random.normal(jax.random.fold_in(_tk, 500 + 20), (125000, 16), jnp.float32)
        tbl_21 = 0.05 * jax.random.normal(jax.random.fold_in(_tk, 500 + 21), (1250, 16), jnp.float32)
        tbl_22 = 0.05 * jax.random.normal(jax.random.fold_in(_tk, 500 + 22), (125000, 16), jnp.float32)
        tbl_23 = 0.05 * jax.random.normal(jax.random.fold_in(_tk, 500 + 23), (12500, 16), jnp.float32)
        tbl_24 = 0.05 * jax.random.normal(jax.random.fold_in(_tk, 500 + 24), (1250, 16), jnp.float32)
        tbl_25 = 0.05 * jax.random.normal(jax.random.fold_in(_tk, 500 + 25), (1000, 16), jnp.float32)
        tbl_26 = 0.05 * jax.random.normal(jax.random.fold_in(_tk, 500 + 26), (1250, 16), jnp.float32)
        tbl_27 = 0.05 * jax.random.normal(jax.random.fold_in(_tk, 500 + 27), (1000, 16), jnp.float32)
        tbl_28 = 0.05 * jax.random.normal(jax.random.fold_in(_tk, 500 + 28), (1000, 16), jnp.float32)
        tbl_29 = 0.05 * jax.random.normal(jax.random.fold_in(_tk, 500 + 29), (125000, 16), jnp.float32)
        tbl_30 = 0.05 * jax.random.normal(jax.random.fold_in(_tk, 500 + 30), (1000, 16), jnp.float32)
        tbl_31 = 0.05 * jax.random.normal(jax.random.fold_in(_tk, 500 + 31), (12500, 16), jnp.float32)
        tbl_32 = 0.05 * jax.random.normal(jax.random.fold_in(_tk, 500 + 32), (12500, 16), jnp.float32)
        tbl_33 = 0.05 * jax.random.normal(jax.random.fold_in(_tk, 500 + 33), (1250, 16), jnp.float32)
        tbl_34 = 0.05 * jax.random.normal(jax.random.fold_in(_tk, 500 + 34), (1250, 16), jnp.float32)
        tbl_35 = 0.05 * jax.random.normal(jax.random.fold_in(_tk, 500 + 35), (1250, 16), jnp.float32)
        tbl_36 = 0.05 * jax.random.normal(jax.random.fold_in(_tk, 500 + 36), (12500, 16), jnp.float32)
        tbl_37 = 0.05 * jax.random.normal(jax.random.fold_in(_tk, 500 + 37), (12500, 16), jnp.float32)
        tbl_38 = 0.05 * jax.random.normal(jax.random.fold_in(_tk, 500 + 38), (12500, 16), jnp.float32)
        _rk = jax.random.fold_in(_tk, 7)
        W_top1 = 0.0606339 * jax.random.normal(jax.random.fold_in(_tk, 801), (272, 512), jnp.float32)
        W_top2 = 0.0441942 * jax.random.normal(jax.random.fold_in(_tk, 802), (512, 256), jnp.float32)
        W_top3 = 0.0625 * jax.random.normal(jax.random.fold_in(_tk, 803), (256, 1), jnp.float32)
        b_top1 = jnp.zeros((512,), jnp.float32)
        b_top2 = jnp.zeros((256,), jnp.float32)
        return (dense_ctx, ids, tbl_0, tbl_1, tbl_2, tbl_3, tbl_4, tbl_5, tbl_6, tbl_7, tbl_8, tbl_9, tbl_10, tbl_11, tbl_12, tbl_13, tbl_14, tbl_15, tbl_16, tbl_17, tbl_18, tbl_19, tbl_20, tbl_21, tbl_22, tbl_23, tbl_24, tbl_25, tbl_26, tbl_27, tbl_28, tbl_29, tbl_30, tbl_31, tbl_32, tbl_33, tbl_34, tbl_35, tbl_36, tbl_37, tbl_38, W_top1, b_top1, W_top2, b_top2, W_top3)
    dense_ctx, ids, tbl_0, tbl_1, tbl_2, tbl_3, tbl_4, tbl_5, tbl_6, tbl_7, tbl_8, tbl_9, tbl_10, tbl_11, tbl_12, tbl_13, tbl_14, tbl_15, tbl_16, tbl_17, tbl_18, tbl_19, tbl_20, tbl_21, tbl_22, tbl_23, tbl_24, tbl_25, tbl_26, tbl_27, tbl_28, tbl_29, tbl_30, tbl_31, tbl_32, tbl_33, tbl_34, tbl_35, tbl_36, tbl_37, tbl_38, W_top1, b_top1, W_top2, b_top2, W_top3 = _rec_inputs()

    def _L0_rec_setup():
        import jax, jax.numpy as jnp
        import numpy as np
        B, F0, D = (256, 39, 16)
        H1, H2 = (128, 128)
        key = jax.random.key(seed)
        k1, k2, k3 = jax.random.split(key, 3)
        x = jax.random.normal(k1, (B, F0, D), dtype=jnp.float32)

        def xavier(k, out_c, in_c):
            bound = np.sqrt(6.0 / (in_c + out_c)).astype(np.float32)
            return jax.random.uniform(k, (out_c, in_c, 1), dtype=jnp.float32, minval=-bound, maxval=bound)
        W0 = xavier(k2, H1, F0 * F0)
        W1 = xavier(k3, H2, F0 * H1)
        return {'input': x, 'W0': W0, 'W1': W1}
    _L0_rec_all = _L0_rec_setup()
    _L0_rec_in = {k: v for k, v in _L0_rec_all.items() if k in ('W0', 'W1')}
    del _L0_rec_all
    return {'dense_ctx': dense_ctx, 'ids': ids, 'tbl_0': tbl_0, 'tbl_1': tbl_1, 'tbl_2': tbl_2, 'tbl_3': tbl_3, 'tbl_4': tbl_4, 'tbl_5': tbl_5, 'tbl_6': tbl_6, 'tbl_7': tbl_7, 'tbl_8': tbl_8, 'tbl_9': tbl_9, 'tbl_10': tbl_10, 'tbl_11': tbl_11, 'tbl_12': tbl_12, 'tbl_13': tbl_13, 'tbl_14': tbl_14, 'tbl_15': tbl_15, 'tbl_16': tbl_16, 'tbl_17': tbl_17, 'tbl_18': tbl_18, 'tbl_19': tbl_19, 'tbl_20': tbl_20, 'tbl_21': tbl_21, 'tbl_22': tbl_22, 'tbl_23': tbl_23, 'tbl_24': tbl_24, 'tbl_25': tbl_25, 'tbl_26': tbl_26, 'tbl_27': tbl_27, 'tbl_28': tbl_28, 'tbl_29': tbl_29, 'tbl_30': tbl_30, 'tbl_31': tbl_31, 'tbl_32': tbl_32, 'tbl_33': tbl_33, 'tbl_34': tbl_34, 'tbl_35': tbl_35, 'tbl_36': tbl_36, 'tbl_37': tbl_37, 'tbl_38': tbl_38, 'W_top1': W_top1, 'b_top1': b_top1, 'W_top2': W_top2, 'b_top2': b_top2, 'W_top3': W_top3, 'L0_rec_W0': _L0_rec_in['W0'], 'L0_rec_W1': _L0_rec_in['W1']}

def reference(dense_ctx, ids, tbl_0, tbl_1, tbl_2, tbl_3, tbl_4, tbl_5, tbl_6, tbl_7, tbl_8, tbl_9, tbl_10, tbl_11, tbl_12, tbl_13, tbl_14, tbl_15, tbl_16, tbl_17, tbl_18, tbl_19, tbl_20, tbl_21, tbl_22, tbl_23, tbl_24, tbl_25, tbl_26, tbl_27, tbl_28, tbl_29, tbl_30, tbl_31, tbl_32, tbl_33, tbl_34, tbl_35, tbl_36, tbl_37, tbl_38, W_top1, b_top1, W_top2, b_top2, W_top3, L0_rec_W0, L0_rec_W1):
    import jax
    import jax.numpy as jnp

    def _L0_rec_ref(input, W0, W1):
        import jax, jax.numpy as jnp
        import numpy as np
        B, F0, D = (256, 39, 16)
        H1, H2 = (128, 128)
        x0 = input
        h = input
        outs = []
        for W in (W0, W1):
            Hout, P, _ = W.shape
            Hk = h.shape[1]
            Wr = W[:, :, 0].reshape(Hout, x0.shape[1], Hk)
            h = jnp.einsum('bfd,bqd,hfq->bhd', x0, h, Wr)
            outs.append(h)
        result = jnp.concatenate(outs, axis=1)
        return jnp.sum(result, axis=2)
    e = jnp.stack([tbl_0[ids[:, 0]], tbl_1[ids[:, 1]], tbl_2[ids[:, 2]], tbl_3[ids[:, 3]], tbl_4[ids[:, 4]], tbl_5[ids[:, 5]], tbl_6[ids[:, 6]], tbl_7[ids[:, 7]], tbl_8[ids[:, 8]], tbl_9[ids[:, 9]], tbl_10[ids[:, 10]], tbl_11[ids[:, 11]], tbl_12[ids[:, 12]], tbl_13[ids[:, 13]], tbl_14[ids[:, 14]], tbl_15[ids[:, 15]], tbl_16[ids[:, 16]], tbl_17[ids[:, 17]], tbl_18[ids[:, 18]], tbl_19[ids[:, 19]], tbl_20[ids[:, 20]], tbl_21[ids[:, 21]], tbl_22[ids[:, 22]], tbl_23[ids[:, 23]], tbl_24[ids[:, 24]], tbl_25[ids[:, 25]], tbl_26[ids[:, 26]], tbl_27[ids[:, 27]], tbl_28[ids[:, 28]], tbl_29[ids[:, 29]], tbl_30[ids[:, 30]], tbl_31[ids[:, 31]], tbl_32[ids[:, 32]], tbl_33[ids[:, 33]], tbl_34[ids[:, 34]], tbl_35[ids[:, 35]], tbl_36[ids[:, 36]], tbl_37[ids[:, 37]], tbl_38[ids[:, 38]]], axis=1)
    z = _L0_rec_ref(e, L0_rec_W0, L0_rec_W1)
    z = z.reshape(z.shape[0], -1)
    h = jnp.concatenate([z, dense_ctx], axis=1)
    h = jnp.maximum(h @ W_top1 + b_top1, 0.0)
    h = jnp.maximum(h @ W_top2 + b_top2, 0.0)
    y = h @ W_top3
    return y

_drawn_inputs = setup_inputs


def setup_inputs(seed=0):
    import zlib

    import numpy as np

    out = dict(_drawn_inputs(seed))
    spreads = {'b_top1': (0.0, 0.1), 'b_top2': (0.0, 0.1)}
    factors = {'tbl_0': 6.76,
     'tbl_1': 6.398,
     'tbl_2': 6.838,
     'tbl_3': 7.022,
     'tbl_4': 7.27,
     'tbl_5': 7.708,
     'tbl_6': 7.002,
     'tbl_7': 7.069,
     'tbl_8': 6.979,
     'tbl_9': 6.932,
     'tbl_10': 6.743,
     'tbl_11': 7.061,
     'tbl_12': 7.395,
     'tbl_13': 7.247,
     'tbl_14': 7.993,
     'tbl_15': 7.722,
     'tbl_16': 6.394,
     'tbl_17': 7.915,
     'tbl_18': 7.041,
     'tbl_19': 7.371,
     'tbl_20': 6.934,
     'tbl_21': 7.444,
     'tbl_22': 7.237,
     'tbl_23': 7.652,
     'tbl_24': 6.323,
     'tbl_25': 6.95,
     'tbl_26': 6.955,
     'tbl_27': 7.48,
     'tbl_28': 7.581,
     'tbl_29': 7.216,
     'tbl_30': 6.747,
     'tbl_31': 6.494,
     'tbl_32': 7.942,
     'tbl_33': 6.637,
     'tbl_34': 7.306,
     'tbl_35': 7.174,
     'tbl_36': 7.321,
     'tbl_37': 6.548,
     'tbl_38': 7.504,
     'L0_rec_W1': 8.0}
    for name, (base, spread) in spreads.items():
        noise = np.random.default_rng([zlib.crc32(name.encode()), seed]).standard_normal(out[name].shape)
        drawn = base * np.exp(spread * noise) if base else spread * noise
        out[name] = jnp.asarray(drawn.astype(out[name].dtype))
    for name, factor in factors.items():
        out[name] = (out[name] * factor).astype(out[name].dtype)
    return out
```

```python
from contextlib import ExitStack

import numpy as np

import concourse.bass as bass
from concourse import mybir

F32 = mybir.dt.float32
BF16 = mybir.dt.bfloat16
I32 = mybir.dt.int32
ALU = mybir.AluOpType
ACT = mybir.ActivationFunctionType

P = 128
BATCH = 512
FIELDS = 39
D = 16
H = 128
QUADS = 4
PER_QUAD = 10
SLOTS = QUADS * PER_QUAD
BLOCK = 32
BLOCKS = BATCH // BLOCK
COLS = BLOCK * D
PARTS = 3
SHIFTS = FIELDS // 2 + 1
PER_TILE = P // FIELDS
TILES = -(-SHIFTS // PER_TILE)
PAIRS = -(-TILES // 2)
GROUP = P // D
GROUPS = BLOCK // GROUP
CHUNK_BLOCKS = 4
CHUNK = CHUNK_BLOCKS * BLOCK
CHUNKS = BATCH // CHUNK
DENSE = 16
TOP1, TOP2 = 512, 256
M1, M2 = TOP1 // P, TOP2 // P
DMAS_IN = 16


def dlrm_cin_tower(nc, table, ids, id_size, id_last, id_base, select, place, ident, w0_ab, w0_ba,
                   w1, wtop1, wtop1_dense, b1, wtop2, b2, wtop3, dense, out):
    with ExitStack() as ctx:
        def sb(name, shape, dt):
            return ctx.enter_context(nc.sbuf_tensor(name, shape, dt))

        def psum(name, shape, dt):
            return ctx.enter_context(nc.psum_tensor(name, shape, dt))

        def sem(name):
            return ctx.enter_context(nc.semaphore(name))

        ids_sb = sb("ids_sb", [P, BLOCKS, PER_QUAD], I32)
        size_sb = sb("size_sb", [P, BLOCKS, PER_QUAD], I32)
        last_sb = sb("last_sb", [P, BLOCKS, PER_QUAD], I32)
        base_sb = sb("base_sb", [P, BLOCKS, PER_QUAD], I32)
        rows_sb = sb("rows_sb", [P, BLOCKS * PER_QUAD], I32)
        select_sb = sb("select_sb", [P, 1 + TILES, P], BF16)
        place_sb = sb("place_sb", [P, SLOTS], BF16)
        ident_sb = sb("ident_sb", [P, P], F32)
        w0_ab_sb = sb("w0_ab_sb", [P, TILES, H], F32)
        w0_ba_sb = sb("w0_ba_sb", [P, TILES, H], F32)
        w0_sb = sb("w0_sb", [P, TILES, H], F32)
        w1_sb = sb("w1_sb", [P, FIELDS, H], F32)
        wtop1_sb = sb("wtop1_sb", [P, 2, TOP1], F32)
        wtop1_dense_sb = sb("wtop1_dense_sb", [DENSE, TOP1], F32)
        wtop2_sb = sb("wtop2_sb", [P, M1, TOP2], F32)
        wtop3_sb = sb("wtop3_sb", [P, M2], F32)
        b1_sb = sb("b1_sb", [P, M1], F32)
        b2_sb = sb("b2_sb", [P, M2], F32)
        dense_sb = sb("dense_sb", [DENSE, BATCH], F32)
        y_sb = sb("y_sb", [1, BATCH], F32)

        chunk_rows = [sb(f"chunk_rows{i}", [P, CHUNK_BLOCKS * PER_QUAD], I32) for i in range(2)]
        emb = [sb(f"emb{i}", [P, PER_QUAD, D], F32) for i in range(2)]
        parts = [sb(f"parts{i}", [P, D, 32], BF16) for i in range(2)]
        rest = sb("rest", [P, D, PER_QUAD], F32)
        stack = [sb(f"stack{i}", [P, D, BLOCK], BF16) for i in range(2)]
        left = [sb(f"left{i}", [P, COLS], F32) for i in range(2)]
        products = [sb(f"products{i}", [P, 2, COLS], F32) for i in range(PAIRS)]
        h1_sb = sb("h1_sb", [P, D, BLOCK], F32)
        h1t_sb = sb("h1t_sb", [P, GROUPS, H], F32)
        emb_rows = [sb(f"emb_rows{i}", [P, GROUPS, SLOTS], F32) for i in range(2)]
        diag = [sb(f"diag{i}", [P, GROUP, GROUPS, SLOTS], F32) for i in range(2)]
        sums = sb("sums", [P, SLOTS, CHUNK], F32)
        z2_sb = sb("z2_sb", [P, CHUNK], F32)
        top1_sb = sb("top1_sb", [P, M1, CHUNK], F32)
        top2_sb = sb("top2_sb", [P, M2, CHUNK], F32)

        right_ps = [psum(f"right_ps{i}", [P, 2, COLS], F32) for i in range(2)]
        h1_ps = psum("h1_ps", [P, COLS], F32)
        turn_ps = psum("turn_ps", [P, COLS], F32)
        sums_ps = [psum(f"sums_ps{i}", [P, 512], F32) for i in range(2)]
        emb_rows_ps = turn_ps[:, 0:GROUPS * SLOTS]

        ids_loaded = sem("ids_loaded")
        select_loaded = sem("select_loaded")
        ident_loaded = sem("ident_loaded")
        w0_loaded = sem("w0_loaded")
        w1_loaded = sem("w1_loaded")
        top_loaded = sem("top_loaded")
        gathered = [sem(f"gathered{i}") for i in range(2)]
        diag_placed = [sem(f"diag_placed{i}") for i in range(2)]
        y_stored = sem("y_stored")
        ids_step = sem("ids_step")
        rows_copied = sem("rows_copied")
        zeroed = sem("zeroed")
        w0_added = sem("w0_added")
        split_step = sem("split_step")
        stack_ready = sem("stack_ready")
        product_ready = sem("product_ready")
        left_done = sem("left_done")
        rows_done = sem("rows_done")
        right_done = sem("right_done")
        layer_done = sem("layer_done")
        turned = sem("turned")
        sums_done = sem("sums_done")
        z2_done = sem("z2_done")
        top1_done = sem("top1_done")
        top2_done = sem("top2_done")
        y_done = sem("y_done")
        left_ready = sem("left_ready")
        emb_rows_ready = sem("emb_rows_ready")
        h1_ready = sem("h1_ready")
        h1t_ready = sem("h1t_ready")
        sums_ready = sem("sums_ready")
        z2_ready = sem("z2_ready")
        top1_ready = sem("top1_ready")
        top2_ready = sem("top2_ready")
        y_ready = sem("y_ready")

        DIAG_DMAS = GROUP * DMAS_IN
        GATHERS = PER_QUAD * DMAS_IN

        block = ctx.enter_context(nc.Block())

        @block.sync
        def _(sp):
            sp.dma_start(ids_sb[:], ids).then_inc(ids_loaded, DMAS_IN)
            sp.dma_start(size_sb[:], id_size).then_inc(ids_loaded, DMAS_IN)
            sp.dma_start(last_sb[:], id_last).then_inc(ids_loaded, DMAS_IN)
            sp.dma_start(base_sb[:], id_base).then_inc(ids_loaded, DMAS_IN)
            sp.dma_start(select_sb[:], select).then_inc(select_loaded, DMAS_IN)
            sp.dma_start(place_sb[:], place).then_inc(select_loaded, DMAS_IN)
            sp.dma_start(w0_ab_sb[:], w0_ab).then_inc(w0_loaded, DMAS_IN)
            sp.dma_start(w0_ba_sb[:], w0_ba).then_inc(w0_loaded, DMAS_IN)
            sp.dma_start(ident_sb[:], ident).then_inc(ident_loaded, DMAS_IN)
            sp.dma_start(w1_sb[:], w1).then_inc(w1_loaded, DMAS_IN)
            sp.dma_start(wtop1_sb[:], wtop1).then_inc(top_loaded, DMAS_IN)
            sp.dma_start(wtop1_dense_sb[:], wtop1_dense).then_inc(top_loaded, DMAS_IN)
            sp.dma_start(b1_sb[:], b1).then_inc(top_loaded, DMAS_IN)
            sp.dma_start(wtop2_sb[:], wtop2).then_inc(top_loaded, DMAS_IN)
            sp.dma_start(b2_sb[:], b2).then_inc(top_loaded, DMAS_IN)
            sp.dma_start(wtop3_sb[:], wtop3).then_inc(top_loaded, DMAS_IN)
            sp.dma_start(dense_sb[:], dense).then_inc(top_loaded, DMAS_IN)
            sp.wait_ge(zeroed, 1)

            def place_diagonal(n, k):
                sp.wait_ge(emb_rows_ready, n + 1)
                for b in range(GROUP):
                    rows = slice(b, P, GROUP)
                    sp.dma_start(diag[k % 2][rows, b], emb_rows[k % 2][rows]) \
                        .then_inc(diag_placed[k % 2], DMAS_IN)

            place_diagonal(0, 0)
            place_diagonal(1, 1)
            with sp.Fori(1, BLOCKS // 2) as i:
                for k in range(2):
                    place_diagonal(2 * i + k, k)
            sp.wait_ge(y_ready, CHUNKS)
            sp.dma_start(out, y_sb[0:1, :]).then_inc(y_stored, DMAS_IN)
            sp.wait_ge(y_stored, DMAS_IN)

        @block.gpsimd
        def _(pool):
            def copy_rows(c, k, first):
                if not first:
                    pool.wait_ge(split_step, 4 * CHUNK_BLOCKS * (c - 1))
                at = bass.ds(c * CHUNK_BLOCKS * PER_QUAD, CHUNK_BLOCKS * PER_QUAD)
                nc.gpsimd.tensor_copy(chunk_rows[k][:], rows_sb[:, at]).then_inc(rows_copied, 1)
                pool.wait_ge(rows_copied, c + 1)

            def gather(n, k, first):
                if not first:
                    pool.wait_ge(split_step, 4 * (n - 1))
                for j in range(PER_QUAD):
                    rows = P if j < PER_QUAD - 1 else P - BLOCK
                    at = (k % CHUNK_BLOCKS) * PER_QUAD + j
                    nc.gpsimd.indirect_dma_start(
                        emb[k % 2][0:rows, j, :], None, table,
                        bass.IndirectOffsetOnAxis(
                            ap=chunk_rows[k // CHUNK_BLOCKS][0:rows, at:at + 1], axis=0),
                    ).then_inc(gathered[k % 2], DMAS_IN)

            pool.wait_ge(ids_step, 4)
            copy_rows(0, 0, True)
            for k in range(CHUNK_BLOCKS):
                gather(k, k, k < 2)
            copy_rows(1, 1, True)
            for k in range(CHUNK_BLOCKS, 2 * CHUNK_BLOCKS):
                gather(k, k, False)
            with pool.Fori(1, CHUNKS // 2) as i:
                for c in range(2):
                    copy_rows(2 * i + c, c, False)
                    for k in range(CHUNK_BLOCKS * c, CHUNK_BLOCKS * (c + 1)):
                        gather(2 * CHUNK_BLOCKS * i + k, k, False)

        @block.vector
        def _(dve):
            dve.wait_ge(ids_loaded, 4 * DMAS_IN)
            nc.vector.scalar_tensor_tensor(size_sb[:], ids_sb[:], 0.0, size_sb[:],
                                           ALU.is_lt, ALU.mult).then_inc(ids_step, 1)
            dve.wait_ge(ids_step, 1)
            nc.vector.tensor_tensor(ids_sb[:], ids_sb[:], size_sb[:], ALU.add).then_inc(ids_step, 1)
            dve.wait_ge(ids_step, 2)
            nc.vector.tensor_tensor(ids_sb[:], ids_sb[:], last_sb[:], ALU.min).then_inc(ids_step, 1)
            dve.wait_ge(ids_step, 3)
            rows_v = rows_sb[:].rearrange("p (n j) -> p n j", j=PER_QUAD)
            nc.vector.scalar_tensor_tensor(rows_v, ids_sb[:], 0.0, base_sb[:],
                                           ALU.max, ALU.add).then_inc(ids_step, 1)
            for i in range(2):
                nc.vector.memset(emb[i][P - BLOCK:P, PER_QUAD - 1, :], 1.0)
                nc.vector.memset(parts[i][:], 0.0)
            nc.vector.memset(diag[0][:], 0.0)
            nc.vector.memset(diag[1][:], 0.0).then_inc(zeroed, 1)
            dve.wait_ge(zeroed, 1)
            dve.wait_ge(w0_loaded, 2 * DMAS_IN)
            nc.vector.tensor_tensor(w0_sb[:], w0_ab_sb[:], w0_ba_sb[:], ALU.add) \
                .then_inc(w0_added, 1)

            def part(k, s):
                return parts[k % 2][:, :, s * PER_QUAD:(s + 1) * PER_QUAD]

            def split(n, k, half, first):
                e = emb[k % 2][:].rearrange("p j d -> p d j")
                dve.wait_ge(gathered[k % 2], GATHERS * (half + 1))
                if n is not None and not first:
                    dve.wait_ge(stack_ready, n - 1)
                nc.vector.tensor_copy(part(k, 0), e).then_inc(split_step, 1)
                dve.wait_ge(split_step, 4 * n + 1)
                nc.vector.tensor_tensor(rest[:], e, part(k, 0), ALU.subtract) \
                    .then_inc(split_step, 1)
                dve.wait_ge(split_step, 4 * n + 2)
                nc.vector.tensor_copy(part(k, 1), rest[:]).then_inc(split_step, 1)
                dve.wait_ge(split_step, 4 * n + 3)
                nc.vector.tensor_tensor(part(k, 2), rest[:], part(k, 1), ALU.subtract) \
                    .then_inc(split_step, 1)
                dve.wait_ge(split_step, 4 * n + 4)
                if not first:
                    dve.wait_ge(right_done, PAIRS * (n - 1))
                nc.vector.transpose(stack[k % 2][:].rearrange("p d b -> p (d b)"),
                                    parts[k % 2][:].rearrange("p d c -> p (d c)")) \
                    .then_inc(stack_ready, 1)

            def multiply(n, k, q, first):
                tiles = min(2, TILES - 2 * q)
                dve.wait_ge(right_done, PAIRS * n + q + 1)
                if q == 0:
                    dve.wait_ge(left_ready, n + 1)
                if not first:
                    dve.wait_ge(layer_done, PAIRS * (n - 1) + q + 1)
                l = left[k % 2][:].rearrange("p (a c) -> p a c", a=1).broadcast_to([P, tiles, COLS])
                nc.vector.tensor_tensor(products[q][:, 0:tiles, :], right_ps[q % 2][:, 0:tiles, :],
                                        l, ALU.mult).then_inc(product_ready, 1)

            def step(n, k, half, first, last=False):
                for q in range(PAIRS):
                    multiply(n, k, q, first)
                if not last:
                    split(n + 1, k + 1, half, first)

            split(0, 0, 0, True)
            step(0, 0, 0, True)
            with dve.Fori(0, CHUNKS - 1) as i:
                for k in range(1, CHUNK_BLOCKS + 1):
                    step(CHUNK_BLOCKS * i + k, k, 2 * i + (k + 1) // 2, False)
            for n in range(BLOCKS - CHUNK_BLOCKS + 1, BLOCKS):
                step(n, n, (n + 1) // 2, False, n == BLOCKS - 1)

        @block.scalar
        def _(act):
            def copy(out_, in_):
                return nc.scalar.activation(out_, in_, ACT.Copy)

            def keep_left(n, k, first):
                act.wait_ge(left_done, n + 1)
                if not first:
                    act.wait_ge(product_ready, PAIRS * (n - 1))
                copy(left[k % 2][:], turn_ps[:]).then_inc(left_ready, 1)

            def keep_emb_rows(n, k, half, first):
                act.wait_ge(rows_done, n + 1)
                if not first:
                    act.wait_ge(diag_placed[k % 2], DIAG_DMAS * half)
                copy(emb_rows[k % 2][:].rearrange("p g f -> p (g f)"), emb_rows_ps) \
                    .then_inc(emb_rows_ready, 1)

            def keep_h1(n, first):
                act.wait_ge(layer_done, PAIRS * (n + 1))
                if not first:
                    act.wait_ge(turned, n)
                copy(h1_sb[:].rearrange("p d b -> p (d b)"), h1_ps[:]).then_inc(h1_ready, 1)

            def keep_h1t(n):
                act.wait_ge(turned, n + 1)
                copy(h1t_sb[:].rearrange("p g h -> p (g h)"), turn_ps[:]).then_inc(h1t_ready, 1)

            def keep_sums(n, k):
                for g in range(GROUPS):
                    at = (k % CHUNK_BLOCKS) * BLOCK + g
                    until = at + BLOCK - GROUPS + 1
                    act.wait_ge(sums_done, GROUPS * n + g + 1)
                    copy(sums[:, :, at:until:GROUPS],
                         sums_ps[g % 2][:, 0:GROUP * SLOTS].rearrange("p (b f) -> p f b", b=GROUP)) \
                        .then_inc(sums_ready, 1)

            def mlp(c):
                act.wait_ge(z2_done, c + 1)
                copy(z2_sb[:], turn_ps[:, 0:CHUNK]).then_inc(z2_ready, 1)
                for m in range(M1):
                    act.wait_ge(top1_done, M1 * c + m + 1)
                    nc.scalar.activation(top1_sb[:, m, :], sums_ps[m % 2][:, 0:CHUNK],
                                         ACT.Relu, bias=b1_sb[:, m:m + 1]).then_inc(top1_ready, 1)
                for m in range(M2):
                    act.wait_ge(top2_done, M2 * c + m + 1)
                    nc.scalar.activation(top2_sb[:, m, :], sums_ps[m][:, 0:CHUNK],
                                         ACT.Relu, bias=b2_sb[:, m:m + 1]).then_inc(top2_ready, 1)
                act.wait_ge(y_done, c + 1)
                copy(y_sb[0:1, bass.ds(c * CHUNK, CHUNK)], turn_ps[0:1, CHUNK:2 * CHUNK]) \
                    .then_inc(y_ready, 1)

            def step(n, k, half, first, last=False):
                if not first:
                    keep_h1t(n - 1)
                    keep_sums(n - 1, k - 1)
                if not last:
                    keep_left(n + 1, k + 1, first)
                keep_h1(n, first)
                if not last:
                    keep_emb_rows(n + 1, k + 1, half, first)

            act.wait_ge(top_loaded, 7 * DMAS_IN)
            keep_left(0, 0, True)
            keep_emb_rows(0, 0, 0, True)
            step(0, 0, 0, True)
            with act.Fori(0, CHUNKS - 1) as i:
                for k in range(1, CHUNK_BLOCKS + 1):
                    step(CHUNK_BLOCKS * i + k, k, 2 * i + (k + 1) // 2, False)
                mlp(i)
            for n in range(BLOCKS - CHUNK_BLOCKS + 1, BLOCKS):
                step(n, n, (n + 1) // 2, False, n == BLOCKS - 1)
            keep_h1t(BLOCKS - 1)
            keep_sums(BLOCKS - 1, BLOCKS - 1)
            mlp(CHUNKS - 1)

        @block.tensor
        def _(pe):
            def place_left(n, k, turns):
                pe.wait_ge(stack_ready, n + 1)
                if turns:
                    pe.wait_ge(h1t_ready, n - 1)
                elif k:
                    pe.wait_ge(emb_rows_ready, 1)
                s = stack[k % 2][:].rearrange("p d b -> p (d b)")
                nc.tensor.matmul(turn_ps[:], select_sb[:, 0, :], s, start=True, stop=True) \
                    .then_inc(left_done, 1)

            def place_rows(n, k):
                pe.wait_ge(left_ready, n + 1)
                for g in range(GROUPS):
                    rows = stack[k % 2][:].rearrange("p d b -> p (d b)")[:, g::GROUPS]
                    last = nc.tensor.matmul(turn_ps[:, g * SLOTS:(g + 1) * SLOTS], rows, place_sb[:],
                                            start=True, stop=True)
                last.then_inc(rows_done, 1)

            def place_right(n, k, q, first):
                if not (first and q < 2):
                    pe.wait_ge(product_ready, PAIRS * n + q - 1)
                s = stack[k % 2][:].rearrange("p d b -> p (d b)")
                for a in range(min(2, TILES - 2 * q)):
                    last = nc.tensor.matmul(right_ps[q % 2][:, a, :],
                                            select_sb[:, 1 + 2 * q + a, :], s,
                                            start=True, stop=True)
                last.then_inc(right_done, 1)

            def layer(n, q, first):
                pe.wait_ge(product_ready, PAIRS * n + q + 1)
                if q == 0 and not first:
                    pe.wait_ge(h1_ready, n)
                for a in range(min(2, TILES - 2 * q)):
                    t = 2 * q + a
                    last = nc.tensor.matmul(h1_ps[:], w0_sb[:, t, :], products[q][:, a, :],
                                            start=(t == 0), stop=(t == TILES - 1))
                last.then_inc(layer_done, 1)

            def turn(n, rows):
                pe.wait_ge(h1_ready, n + 1)
                pe.wait_ge(emb_rows_ready, rows)
                for g in range(GROUPS):
                    cols = h1_sb[:].rearrange("p d b -> p (d b)")[:, g::GROUPS]
                    last = nc.tensor.transpose(turn_ps[:, g * H:(g + 1) * H], cols, ident_sb[:])
                last.then_inc(turned, 1)

            def sum_over_d(n, k, half):
                pe.wait_ge(h1t_ready, n + 1)
                pe.wait_ge(diag_placed[k % 2], DIAG_DMAS * (half + 1))
                for g in range(GROUPS):
                    if g >= 2:
                        pe.wait_ge(sums_ready, GROUPS * n + g - 1)
                    nc.tensor.matmul(sums_ps[g % 2][:, 0:GROUP * SLOTS], h1t_sb[:, g, :],
                                     diag[k % 2][:, :, g, :], start=True, stop=True) \
                        .then_inc(sums_done, 1)

            def chunk(c, rows):
                pe.wait_ge(sums_ready, GROUPS * CHUNK_BLOCKS * (c + 1))
                pe.wait_ge(emb_rows_ready, rows)
                for f in range(FIELDS):
                    last = nc.tensor.matmul(turn_ps[:, 0:CHUNK], w1_sb[:, f, :], sums[:, f, :],
                                            start=(f == 0), stop=(f == FIELDS - 1))
                last.then_inc(z2_done, 1)
                for m in range(M1):
                    cols = slice(m * P, (m + 1) * P)
                    u = sums_ps[m % 2][:, 0:CHUNK]
                    if m >= 2:
                        pe.wait_ge(top1_ready, M1 * c + m - 1)
                    nc.tensor.matmul(u, wtop1_sb[:, 0, cols], sums[:, FIELDS, :],
                                     start=True, stop=False)
                    nc.tensor.matmul(u, wtop1_dense_sb[:, cols],
                                     dense_sb[:, bass.ds(c * CHUNK, CHUNK)],
                                     start=False, stop=False)
                    if m == 0:
                        pe.wait_ge(z2_ready, c + 1)
                    nc.tensor.matmul(u, wtop1_sb[:, 1, cols], z2_sb[:], start=False, stop=True) \
                        .then_inc(top1_done, 1)
                pe.wait_ge(top1_ready, M1 * c + M1 - 1)
                for m in range(M2):
                    for j in range(M1):
                        if m == 0 and j == M1 - 1:
                            pe.wait_ge(top1_ready, M1 * c + M1)
                        last = nc.tensor.matmul(sums_ps[m][:, 0:CHUNK],
                                                wtop2_sb[:, j, m * P:(m + 1) * P], top1_sb[:, j, :],
                                                start=(j == 0), stop=(j == M1 - 1))
                    last.then_inc(top2_done, 1)
                for m in range(M2):
                    pe.wait_ge(top2_ready, M2 * c + m + 1)
                    last = nc.tensor.matmul(turn_ps[0:1, CHUNK:2 * CHUNK], wtop3_sb[:, m:m + 1],
                                            top2_sb[:, m, :], start=(m == 0), stop=(m == M2 - 1))
                last.then_inc(y_done, 1)
                pe.wait_ge(y_ready, c + 1)

            def step(n, k, half, first, last=False):
                layer(n, 0, first)
                if not first:
                    turn(n - 1, n + 1)
                place_right(n, k, 2, first)
                layer(n, 1, first)
                place_right(n, k, 3, first)
                layer(n, 2, first)
                if not first:
                    sum_over_d(n - 1, k - 1, half)
                if not last:
                    place_left(n + 1, k + 1, not first)
                    place_right(n + 1, k + 1, 0, False)
                layer(n, 3, first)
                if not last:
                    place_rows(n + 1, k + 1)
                    place_right(n + 1, k + 1, 1, False)

            pe.wait_ge(select_loaded, 2 * DMAS_IN)
            place_left(0, 0, False)
            place_rows(0, 0)
            place_right(0, 0, 0, True)
            place_right(0, 0, 1, True)
            pe.wait_ge(w0_added, 1)
            step(0, 0, 0, True)
            pe.wait_ge(ident_loaded, DMAS_IN)
            pe.wait_ge(w1_loaded, DMAS_IN)
            pe.wait_ge(top_loaded, 7 * DMAS_IN)
            with pe.Fori(0, CHUNKS - 1) as i:
                for k in range(1, CHUNK_BLOCKS + 1):
                    step(CHUNK_BLOCKS * i + k, k, 2 * i + (k - 1) // 2, False)
                chunk(i, CHUNK_BLOCKS * (i + 1) + 2)
            for n in range(BLOCKS - CHUNK_BLOCKS + 1, BLOCKS):
                step(n, n, (n - 1) // 2, False, n == BLOCKS - 1)
            turn(BLOCKS - 1, BLOCKS)
            sum_over_d(BLOCKS - 1, BLOCKS - 1, BLOCKS // 2 - 1)
            chunk(CHUNKS - 1, BLOCKS)


def field_of(i, j):
    f = PER_QUAD * i + j
    return f if f < FIELDS else None


def shape_constants(table_rows):
    base = np.concatenate([[0], np.cumsum(table_rows)[:-1]])
    size = np.zeros((P, BLOCKS, PER_QUAD), np.int32)
    last, first_row = size.copy(), size.copy()
    select = np.zeros((P, 1 + TILES, P), np.float32)
    place = np.zeros((P, SLOTS), np.float32)
    for i in range(QUADS):
        for j in range(PER_QUAD):
            f = field_of(i, j)
            for s in range(PARTS):
                row = 32 * i + s * PER_QUAD + j
                place[row, PER_QUAD * i + j] = 1.0
                if f is None:
                    continue
                for g in range(PER_TILE):
                    select[row, 0, g * FIELDS + f] = 1.0
                    for t in range(TILES):
                        shift = PER_TILE * t + g
                        if shift < SHIFTS:
                            select[row, 1 + t, g * FIELDS + (f - shift) % FIELDS] = 1.0
            if f is not None:
                quad = slice(32 * i, 32 * i + 32)
                size[quad, :, j] = table_rows[f]
                last[quad, :, j] = table_rows[f] - 1
                first_row[quad, :, j] = base[f]
    return size, last, first_row, select, place


def kernel(**inputs):
    import ml_dtypes
    import concourse.bacc as bacc
    from concourse.bass_utils import run_bass_kernel_spmd

    x = {name: np.asarray(a) for name, a in inputs.items()}
    tables = [x[f"tbl_{f}"] for f in range(FIELDS)]
    size, last, first_row, select, place = shape_constants([t.shape[0] for t in tables])

    ids = np.zeros((P, BLOCKS, PER_QUAD), np.int32)
    by_block = x["ids"].reshape(BLOCKS, BLOCK, FIELDS)
    for i in range(QUADS):
        for j in range(PER_QUAD):
            if field_of(i, j) is not None:
                ids[32 * i:32 * i + 32, :, j] = by_block[:, :, field_of(i, j)].T

    w0 = x["L0_rec_W0"].reshape(H, FIELDS, FIELDS)
    w0_ab = np.zeros((P, TILES, H), np.float32)
    w0_ba = np.zeros((P, TILES, H), np.float32)
    j = np.arange(FIELDS)
    for shift in range(SHIFTS):
        t, g = divmod(shift, PER_TILE)
        rows = slice(g * FIELDS, (g + 1) * FIELDS)
        w0_ab[rows, t] = w0[:, j, (j + shift) % FIELDS].T
        if shift:
            w0_ba[rows, t] = w0[:, (j + shift) % FIELDS, j].T

    arrays = {
        "table": np.concatenate(tables, axis=0),
        "ids": ids,
        "id_size": size,
        "id_last": last,
        "id_base": first_row,
        "select": select.astype(ml_dtypes.bfloat16),
        "place": place.astype(ml_dtypes.bfloat16),
        "ident": np.eye(P, dtype=np.float32),
        "w0_ab": w0_ab,
        "w0_ba": w0_ba,
        "w1": x["L0_rec_W1"].reshape(H, FIELDS, H).transpose(2, 1, 0),
        "wtop1": x["W_top1"][:2 * H].reshape(2, H, TOP1).transpose(1, 0, 2),
        "wtop1_dense": x["W_top1"][2 * H:],
        "b1": x["b_top1"].reshape(M1, P).T,
        "wtop2": x["W_top2"].reshape(M1, P, TOP2).transpose(1, 0, 2),
        "b2": x["b_top2"].reshape(M2, P).T,
        "wtop3": x["W_top3"].reshape(M2, P).T,
        "dense": x["dense_ctx"].T,
    }
    arrays = {name: np.ascontiguousarray(a) for name, a in arrays.items()}
    nc = bacc.Bacc("TRN2", target_bir_lowering=False, num_devices=1)
    args = [nc.dram_tensor(name, a.shape, mybir.dt.from_np(a.dtype), kind="ExternalInput").ap()
            for name, a in arrays.items()]
    out = nc.dram_tensor("y", (1, BATCH), F32, kind="ExternalOutput").ap()
    dlrm_cin_tower(nc, *args, out)
    r = run_bass_kernel_spmd(nc, [arrays], core_ids=[0])
    return r.results[0]["y"].reshape(BATCH, 1)
```

```python
from contextlib import ExitStack

import numpy as np

import concourse.bass as bass
from concourse import mybir

F32 = mybir.dt.float32
F32R = mybir.dt.float32r
BF16 = mybir.dt.bfloat16
I32 = mybir.dt.int32
ALU = mybir.AluOpType
ACT = mybir.ActivationFunctionType

P = 128
BATCH = 512
FIELDS = 39
D = 16
H = 128
QUADS = 4
PER_QUAD = 10
SLOTS = QUADS * PER_QUAD
BLOCK = 32
BLOCKS = BATCH // BLOCK
COLS = BLOCK * D
PARTS = 3
PAIRS = FIELDS * (FIELDS + 1) // 2
FULL_TILES = PAIRS // P
TILES = FULL_TILES + 1
HI_HI, LO_HI, HI_LO = slice(0, 64), slice(64, 96), slice(96, P)
STEPS = -(-TILES // 2)
GROUP = P // D
GROUPS = BLOCK // GROUP
CHUNK_BLOCKS = 4
CHUNK = CHUNK_BLOCKS * BLOCK
CHUNKS = BATCH // CHUNK
DENSE = 16
TOP1, TOP2 = 512, 256
M1, M2 = TOP1 // P, TOP2 // P
Z2_CUTS = (0, 4, 6, FIELDS // 3)
EARLY = 1
DMAS_IN = 16


def dlrm_cin_tower(nc, table, id_data, select, place, ident, w0_ab, w0_ba,
                   w1, wtop1, wtop1_dense, b1, wtop2, b2, wtop3, dense, out):
    with ExitStack() as ctx:
        def sb(name, shape, dt):
            return ctx.enter_context(nc.sbuf_tensor(name, shape, dt))

        def psum(name, shape, dt):
            return ctx.enter_context(nc.psum_tensor(name, shape, dt))

        def sem(name):
            return ctx.enter_context(nc.semaphore(name))

        id_data_sb = sb("id_data_sb", [P, 4, BLOCKS, PER_QUAD], I32)
        rows_sb = sb("rows_sb", [P, (BLOCKS - CHUNK_BLOCKS) * PER_QUAD], I32)
        select_sb = sb("select_sb", [P, 1 + TILES, P], BF16)
        place_sb = sb("place_sb", [P, SLOTS], BF16)
        ident_sb = sb("ident_sb", [P, P], F32)
        w0_ab_sb = sb("w0_ab_sb", [P, TILES, H], F32)
        w0_ba_sb = sb("w0_ba_sb", [P, TILES, H], F32)
        w0_sb = sb("w0_sb", [P, TILES, H], F32)
        w0_hi = sb("w0_hi", [P, TILES, H], F32R)
        w0_lo = sb("w0_lo", [P, TILES, H], F32R)
        w1_sb = sb("w1_sb", [P, FIELDS, H], F32)
        wtop1_sb = sb("wtop1_sb", [P, 2, TOP1], F32)
        wtop1_dense_sb = sb("wtop1_dense_sb", [DENSE, TOP1], F32)
        wtop2_sb = sb("wtop2_sb", [P, M1, TOP2], F32)
        wtop3_sb = sb("wtop3_sb", [P, M2], F32)
        b1_sb = sb("b1_sb", [P, M1], F32)
        b2_sb = sb("b2_sb", [P, M2], F32)
        dense_sb = sb("dense_sb", [DENSE, BATCH], F32)
        y_sb = sb("y_sb", [1, BATCH], F32)

        chunk_rows = [sb(f"chunk_rows{i}", [P, CHUNK_BLOCKS * PER_QUAD], I32) for i in range(2)]
        emb = [sb(f"emb{i}", [P, PER_QUAD, D], F32) for i in range(CHUNK_BLOCKS)]
        parts = [sb(f"parts{i}", [P, D, 32], BF16) for i in range(2)]
        rest = sb("rest", [P, D, PER_QUAD], F32)
        stack = [sb(f"stack{i}", [P, D, BLOCK], BF16) for i in range(2)]
        left = [sb(f"left{i}", [P, COLS], F32) for i in range(2)]
        products = [sb(f"products{i}", [P, 2, COLS], F32) for i in range(STEPS)]
        products_hi = [sb(f"products_hi{i}", [P, 2, COLS], F32R) for i in range(STEPS)]
        products_lo = [sb(f"products_lo{i}", [P, 2, COLS], F32R) for i in range(STEPS - 1)]
        h1_sb = sb("h1_sb", [P, D, BLOCK], F32)
        h1t_hi = sb("h1t_hi", [P, GROUPS, H], F32R)
        h1t_lo = sb("h1t_lo", [P, GROUPS, H], F32R)
        emb_rows = [sb(f"emb_rows{i}", [P, 2, GROUPS, SLOTS], F32R) for i in range(2)]
        diag = [sb(f"diag{i}", [P, GROUP, 2, GROUPS, SLOTS], F32R) for i in range(2)]
        sums = sb("sums", [P, 2, SLOTS, CHUNK], F32)
        z2_sb = sb("z2_sb", [P, CHUNK], F32)
        top1_sb = sb("top1_sb", [P, M1, CHUNK], F32)
        top2_sb = sb("top2_sb", [P, M2, CHUNK], F32)

        right_ps = [psum(f"right_ps{i}", [P, 2, COLS], F32) for i in range(2)]
        h1_ps = psum("h1_ps", [P, COLS], F32)
        turn_ps = psum("turn_ps", [P, COLS], F32)
        sums_ps = psum("sums_ps", [P, 512], F32)
        top_ps = psum("top_ps", [P, 512], F32)
        emb_rows_ps = turn_ps[:, 0:GROUPS * SLOTS]

        ids_loaded = sem("ids_loaded")
        select_loaded = sem("select_loaded")
        ident_loaded = sem("ident_loaded")
        w0_loaded = sem("w0_loaded")
        w1_loaded = sem("w1_loaded")
        top_loaded = sem("top_loaded")
        gathered = [sem(f"gathered{i}") for i in range(CHUNK_BLOCKS)]
        diag_placed = [sem(f"diag_placed{i}") for i in range(2)]
        y_stored = sem("y_stored")
        ids_step = sem("ids_step")
        rows_copied = sem("rows_copied")
        zeroed = sem("zeroed")
        w0_step = sem("w0_step")
        first_part = sem("first_part")
        second_part = sem("second_part")
        rest_ready = sem("rest_ready")
        third_part = sem("third_part")
        stack_ready = sem("stack_ready")
        product_ready = sem("product_ready")
        hi_ready = sem("hi_ready")
        lo_ready = sem("lo_ready")
        left_done = sem("left_done")
        rows_done = sem("rows_done")
        right_done = sem("right_done")
        layer_done = sem("layer_done")
        turned = sem("turned")
        sums_done = sem("sums_done")
        z2_done = sem("z2_done")
        top1_done = sem("top1_done")
        top2_done = sem("top2_done")
        y_done = sem("y_done")
        left_ready = sem("left_ready")
        rows_hi_ready = sem("rows_hi_ready")
        rows_lo_ready = sem("rows_lo_ready")
        h1_ready = sem("h1_ready")
        h1t_hi_ready = sem("h1t_hi_ready")
        h1t_lo_ready = sem("h1t_lo_ready")
        sums_ready = sem("sums_ready")
        last_sums_ready = sem("last_sums_ready")
        z2_ready = sem("z2_ready")
        top1_ready = sem("top1_ready")
        top2_ready = sem("top2_ready")
        y_ready = sem("y_ready")

        DIAG_DMAS = GROUP * DMAS_IN
        GATHERS = PER_QUAD * DMAS_IN

        def part(k, s):
            return parts[k % 2][:, :, s * PER_QUAD:(s + 1) * PER_QUAD]

        def last_sums(g):
            return (sums_ps, h1_ps, turn_ps, sums_ps)[g][:, 0:GROUP * SLOTS]

        def last_top1(m):
            return right_ps[m // 2][:, m % 2, 0:CHUNK]

        def last_top2(m):
            return (turn_ps, top_ps)[m][:, 0:CHUNK]

        last_z2 = h1_ps[:, 0:CHUNK]
        last_y = sums_ps[0:1, 0:CHUNK]

        def copy_sums_args(k, c, g, ps):
            at = (k % CHUNK_BLOCKS) * BLOCK + g
            return (sums[:, c % 2, :, at:at + BLOCK - GROUPS + 1:GROUPS],
                    ps.rearrange("p (b f) -> p f b", b=GROUP))

        def tiles_of(q):
            return min(2, TILES - 2 * q)

        block = ctx.enter_context(nc.Block())

        @block.sync
        def _(sp):
            sp.dma_start(id_data_sb[:], id_data).then_inc(ids_loaded, DMAS_IN)
            sp.dma_start(select_sb[:], select).then_inc(select_loaded, DMAS_IN)
            sp.dma_start(place_sb[:], place).then_inc(select_loaded, DMAS_IN)
            sp.dma_start(w0_ab_sb[:], w0_ab).then_inc(w0_loaded, DMAS_IN)
            sp.dma_start(w0_ba_sb[:], w0_ba).then_inc(w0_loaded, DMAS_IN)
            sp.dma_start(ident_sb[:], ident).then_inc(ident_loaded, DMAS_IN)
            sp.dma_start(w1_sb[:], w1).then_inc(w1_loaded, DMAS_IN)
            sp.dma_start(wtop1_sb[:], wtop1).then_inc(top_loaded, DMAS_IN)
            sp.dma_start(wtop1_dense_sb[:], wtop1_dense).then_inc(top_loaded, DMAS_IN)
            sp.dma_start(b1_sb[:], b1).then_inc(top_loaded, DMAS_IN)
            sp.dma_start(wtop2_sb[:], wtop2).then_inc(top_loaded, DMAS_IN)
            sp.dma_start(b2_sb[:], b2).then_inc(top_loaded, DMAS_IN)
            sp.dma_start(wtop3_sb[:], wtop3).then_inc(top_loaded, DMAS_IN)
            sp.dma_start(dense_sb[:], dense).then_inc(top_loaded, DMAS_IN)
            sp.wait_ge(zeroed, 1)

            def place_diagonal(n, k):
                sp.wait_ge(rows_lo_ready, n + 1)
                for b in range(GROUP):
                    rows = slice(b, P, GROUP)
                    sp.dma_start(diag[k % 2][rows, b].bitcast(F32),
                                 emb_rows[k % 2][rows].bitcast(F32)) \
                        .then_inc(diag_placed[k % 2], DMAS_IN)

            place_diagonal(0, 0)
            place_diagonal(1, 1)
            with sp.Fori(1, BLOCKS // 2) as i:
                for k in range(2):
                    place_diagonal(2 * i + k, k)
            sp.wait_ge(y_ready, CHUNKS)
            sp.dma_start(out, y_sb[0:1, :]).then_inc(y_stored, DMAS_IN)
            sp.wait_ge(y_stored, DMAS_IN)

        @block.gpsimd
        def _(pool):
            def copy_rows(c, k, first):
                if not first:
                    pool.wait_ge(rest_ready, CHUNK_BLOCKS * (c - 1))
                at = bass.ds((c - 1) * CHUNK_BLOCKS * PER_QUAD, CHUNK_BLOCKS * PER_QUAD)
                nc.gpsimd.tensor_copy(chunk_rows[k][:], rows_sb[:, at]).then_inc(rows_copied, 1)
                pool.wait_ge(rows_copied, c)

            def gather(n, j_chunk, k, first):
                if not first:
                    pool.wait_ge(rest_ready, n - CHUNK_BLOCKS + 1)
                for j in range(PER_QUAD):
                    rows = P if j < PER_QUAD - 1 else P - BLOCK
                    at = k * PER_QUAD + j
                    nc.gpsimd.indirect_dma_start(
                        emb[k][0:rows, j, :], None, table,
                        bass.IndirectOffsetOnAxis(ap=chunk_rows[j_chunk][0:rows, at:at + 1], axis=0),
                    ).then_inc(gathered[k], DMAS_IN)

            pool.wait_ge(ids_step, 4)
            for c in range(2):
                if c:
                    pool.wait_ge(ids_step, 8)
                    copy_rows(c, c, True)
                for k in range(CHUNK_BLOCKS):
                    gather(CHUNK_BLOCKS * c + k, c, k, c == 0)
            with pool.Fori(1, CHUNKS // 2) as i:
                for c in range(2):
                    copy_rows(2 * i + c, c, False)
                    for k in range(CHUNK_BLOCKS):
                        gather(CHUNK_BLOCKS * (2 * i + c) + k, c, k, False)

        @block.vector
        def _(dve):
            dve.wait_ge(ids_loaded, DMAS_IN)

            def number_rows(blocks, out_, steps):
                ids, size, last, base = (id_data_sb[:, i, blocks, :] for i in range(4))
                nc.vector.scalar_tensor_tensor(size, ids, 0.0, size, ALU.is_lt, ALU.mult) \
                    .then_inc(ids_step, 1)
                dve.wait_ge(ids_step, steps + 1)
                nc.vector.tensor_tensor(ids, ids, size, ALU.add).then_inc(ids_step, 1)
                dve.wait_ge(ids_step, steps + 2)
                nc.vector.tensor_tensor(ids, ids, last, ALU.min).then_inc(ids_step, 1)
                dve.wait_ge(ids_step, steps + 3)
                nc.vector.scalar_tensor_tensor(out_[:].rearrange("p (n j) -> p n j", j=PER_QUAD),
                                               ids, 0.0, base, ALU.max, ALU.add).then_inc(ids_step, 1)

            number_rows(slice(0, CHUNK_BLOCKS), chunk_rows[0], 0)
            number_rows(slice(CHUNK_BLOCKS, BLOCKS), rows_sb, 4)
            for e in emb:
                nc.vector.memset(e[P - BLOCK:P, PER_QUAD - 1, :], 1.0)
            for i in range(2):
                nc.vector.memset(parts[i][:], 0.0)
            nc.vector.memset(diag[0][:].bitcast(F32), 0.0)
            nc.vector.memset(diag[1][:].bitcast(F32), 0.0).then_inc(zeroed, 1)
            dve.wait_ge(zeroed, 1)
            dve.wait_ge(w0_loaded, 2 * DMAS_IN)
            nc.vector.tensor_tensor(w0_sb[:], w0_ab_sb[:], w0_ba_sb[:], ALU.add) \
                .then_inc(w0_step, 1)
            dve.wait_ge(w0_step, 1)
            nc.vector.tensor_copy(w0_hi[:], w0_sb[:]).then_inc(w0_step, 1)
            dve.wait_ge(w0_step, 2)
            nc.vector.tensor_tensor(w0_lo[:], w0_sb[:], w0_hi[:].bitcast(F32), ALU.subtract) \
                .then_inc(w0_step, 1)
            dve.wait_ge(w0_step, 3)
            nc.vector.tensor_copy(w0_hi[LO_HI, TILES - 1, :], w0_lo[LO_HI, TILES - 1, :]) \
                .then_inc(w0_step, 1)

            def take_rest(n, k, first):
                dve.wait_ge(first_part, n + 1)
                if not first:
                    dve.wait_ge(third_part, n)
                nc.vector.tensor_tensor(rest[:], emb[k % CHUNK_BLOCKS][:].rearrange("p j d -> p d j"),
                                        part(k, 0), ALU.subtract).then_inc(rest_ready, 1)

            def take_third(n, k):
                dve.wait_ge(second_part, n + 1)
                nc.vector.tensor_tensor(part(k, 2), rest[:], part(k, 1), ALU.subtract) \
                    .then_inc(third_part, 1)

            def stack_parts(n, k, first):
                dve.wait_ge(third_part, n + 1)
                if not first:
                    dve.wait_ge(right_done, STEPS * (n - 1))
                nc.vector.transpose(stack[k % 2][:].rearrange("p d b -> p (d b)"),
                                    parts[k % 2][:].rearrange("p d c -> p (d c)")) \
                    .then_inc(stack_ready, 1)

            def multiply(n, k, q, first):
                tiles = tiles_of(q)
                dve.wait_ge(right_done, STEPS * n + q + 1)
                if q == 0:
                    dve.wait_ge(left_ready, n + 1)
                if not first:
                    dve.wait_ge(lo_ready, STEPS * (n - 1) + q + 1)
                l = left[k % 2][:].rearrange("p (a c) -> p a c", a=1).broadcast_to([P, tiles, COLS])
                nc.vector.tensor_tensor(products[q][:, 0:tiles, :], right_ps[q % 2][:, 0:tiles, :],
                                        l, ALU.mult).then_inc(product_ready, 1)

            def take_lo(n, q, first):
                tiles = tiles_of(q)
                dve.wait_ge(hi_ready, STEPS * n + q + 1)
                if not first:
                    dve.wait_ge(layer_done, STEPS * (n - 1) + q + 1)
                rows = HI_LO if q == STEPS - 1 else slice(0, P)
                lo = products_hi[q] if q == STEPS - 1 else products_lo[q]
                nc.vector.tensor_tensor(lo[rows, 0:tiles, :], products[q][rows, 0:tiles, :],
                                        products_hi[q][rows, 0:tiles, :].bitcast(F32),
                                        ALU.subtract).then_inc(lo_ready, 1)

            def take_rows_lo(n, k):
                dve.wait_ge(rows_hi_ready, n + 1)
                rows = [emb_rows[k % 2][:, s].rearrange("p g f -> p (g f)") for s in range(2)]
                nc.vector.tensor_tensor(rows[1], emb_rows_ps, rows[0].bitcast(F32), ALU.subtract) \
                    .then_inc(rows_lo_ready, 1)

            def take_h1t_lo(n):
                dve.wait_ge(h1t_hi_ready, n + 1)
                hi, lo = (t[:].rearrange("p g h -> p (g h)") for t in (h1t_hi, h1t_lo))
                nc.vector.tensor_tensor(lo, turn_ps[:], hi.bitcast(F32), ALU.subtract) \
                    .then_inc(h1t_lo_ready, 1)

            def split(n, k, first):
                take_rest(n, k, first)
                take_third(n, k)
                stack_parts(n, k, isinstance(n, int) and n < 2)

            def start_products(n, k, first):
                multiply(n, k, 1, first)
                take_lo(n, 0, first)
                if first:
                    multiply(n, k, 2, first)
                take_lo(n, 1, first)
                if first:
                    multiply(n, k, 3, first)
                take_rows_lo(n, k)

            def early_step(n):
                for q in (2, 3):
                    take_lo(n, q, n == 0)
                if n:
                    take_h1t_lo(n - 1)
                split(n + 1, n + 1, False)
                multiply(n + 1, n + 1, 0, False)
                start_products(n + 1, n + 1, False)

            def step(n, k, more=2):
                multiply(n, k, 2, False)
                take_h1t_lo(n - 1)
                multiply(n, k, 3, False)
                take_lo(n, 2, False)
                if more:
                    multiply(n + 1, k + 1, 0, False)
                take_lo(n, 3, False)
                if more:
                    multiply(n + 1, k + 1, 1, False)
                    take_lo(n + 1, 0, False)
                if more > 1:
                    take_rest(n + 2, k + 2, False)
                if more:
                    take_lo(n + 1, 1, False)
                    take_rows_lo(n + 1, k + 1)
                if more > 1:
                    take_third(n + 2, k + 2)
                    stack_parts(n + 2, k + 2, False)

            split(0, 0, True)
            multiply(0, 0, 0, True)
            start_products(0, 0, True)
            for n in range(EARLY):
                early_step(n)
            split(EARLY + 1, EARLY + 1, False)
            for n in range(EARLY, CHUNK_BLOCKS + 1):
                step(n, n)
            with dve.Fori(1, CHUNKS - 1) as i:
                for k in range(1, CHUNK_BLOCKS + 1):
                    step(CHUNK_BLOCKS * i + k, k)
            for n in range(BLOCKS - CHUNK_BLOCKS + 1, BLOCKS):
                step(n, n, BLOCKS - 1 - n)
            take_h1t_lo(BLOCKS - 1)
            for g in (1, 3):
                dve.wait_ge(sums_done, GROUPS * (BLOCKS - 1) + g + 1)
                nc.vector.tensor_copy(*copy_sums_args(BLOCKS - 1, CHUNKS - 1, g, last_sums(g))) \
                    .then_inc(last_sums_ready, 1)

        @block.scalar
        def _(act):
            def copy(out_, in_):
                return nc.scalar.activation(out_, in_, ACT.Copy)

            def take_first(n, k, use, first):
                act.wait_ge(gathered[k % CHUNK_BLOCKS], GATHERS * (use + 1))
                if first:
                    act.wait_ge(zeroed, 1)
                else:
                    act.wait_ge(stack_ready, n - 1)
                copy(part(k, 0), emb[k % CHUNK_BLOCKS][:].rearrange("p j d -> p d j")).then_inc(first_part, 1)

            def take_second(n, k):
                act.wait_ge(rest_ready, n + 1)
                copy(part(k, 1), rest[:]).then_inc(second_part, 1)

            def take_hi(n, q, first):
                tiles = tiles_of(q)
                act.wait_ge(product_ready, STEPS * n + q + 1)
                if not first:
                    act.wait_ge(layer_done, STEPS * (n - 1) + q + 1)
                copy(products_hi[q][:, 0:tiles, :], products[q][:, 0:tiles, :]).then_inc(hi_ready, 1)

            def keep_left(n, k, first):
                act.wait_ge(left_done, n + 1)
                if not first:
                    act.wait_ge(product_ready, STEPS * (n - 1))
                copy(left[k % 2][:], turn_ps[:]).then_inc(left_ready, 1)

            def take_rows_hi(n, k, half, first):
                act.wait_ge(rows_done, n + 1)
                if not first:
                    act.wait_ge(diag_placed[k % 2], DIAG_DMAS * half)
                copy(emb_rows[k % 2][:, 0].rearrange("p g f -> p (g f)"), emb_rows_ps) \
                    .then_inc(rows_hi_ready, 1)

            def keep_h1(n, first):
                act.wait_ge(layer_done, STEPS * (n + 1))
                if not first:
                    act.wait_ge(turned, n)
                copy(h1_sb[:].rearrange("p d b -> p (d b)"), h1_ps[:]).then_inc(h1_ready, 1)

            def take_h1t_hi(n):
                act.wait_ge(turned, n + 1)
                copy(h1t_hi[:].rearrange("p g h -> p (g h)"), turn_ps[:]).then_inc(h1t_hi_ready, 1)

            def keep_sums(n, k, c, groups):
                for g in groups:
                    act.wait_ge(sums_done, GROUPS * n + g + 1)
                    copy(*copy_sums_args(k, c, g, sums_ps[:, 0:GROUP * SLOTS])).then_inc(sums_ready, 1)

            def keep_z2(c):
                act.wait_ge(z2_done, c + 1)
                copy(z2_sb[:], top_ps[:, 0:CHUNK]).then_inc(z2_ready, 1)

            def keep_top1(c):
                act.wait_ge(top1_done, c + 1)
                for m in range(M1):
                    nc.scalar.activation(top1_sb[:, m, :], top_ps[:, m * CHUNK:(m + 1) * CHUNK],
                                         ACT.Relu, bias=b1_sb[:, m:m + 1]).then_inc(top1_ready, 1)

            def keep_top2(c):
                act.wait_ge(top2_done, c + 1)
                for m in range(M2):
                    nc.scalar.activation(top2_sb[:, m, :], top_ps[:, m * CHUNK:(m + 1) * CHUNK],
                                         ACT.Relu, bias=b2_sb[:, m:m + 1]).then_inc(top2_ready, 1)

            def keep_y(c):
                act.wait_ge(y_done, c + 1)
                copy(y_sb[0:1, bass.ds(c * CHUNK, CHUNK)], top_ps[0:1, 0:CHUNK]).then_inc(y_ready, 1)

            def split(n, k, use, first):
                take_first(n, k, use, first)
                take_second(n, k)

            def early_step(n):
                take_hi(n, 2, n == 0)
                take_hi(n, 3, n == 0)
                if n:
                    take_h1t_hi(n - 1)
                    keep_sums(n - 1, n - 1, 0, range(GROUPS))
                keep_h1(n, n == 0)
                split(n + 1, n + 1, 0, n == 0)
                keep_left(n + 1, n + 1, n == 0)
                take_hi(n + 1, 0, False)
                take_hi(n + 1, 1, False)
                take_rows_hi(n + 1, n + 1, (n + 1) // 2, n == 0)

            def step(n, k, half, sums_c, c, more=2):
                mlp = c is not None and k % CHUNK_BLOCKS == 0
                take_h1t_hi(n - 1)
                if mlp:
                    keep_top1(c)
                take_hi(n, 2, False)
                if more:
                    keep_left(n + 1, k + 1, False)
                take_hi(n, 3, False)
                keep_sums(n - 1, k - 1, sums_c, [0])
                if more:
                    take_hi(n + 1, 0, False)
                keep_sums(n - 1, k - 1, sums_c, [1])
                if mlp:
                    keep_top2(c)
                if more:
                    take_hi(n + 1, 1, False)
                if more > 1:
                    take_first(n + 2, k + 2, sums_c + (k + 2) // CHUNK_BLOCKS, False)
                keep_sums(n - 1, k - 1, sums_c, [2])
                if mlp:
                    keep_y(c)
                if c is not None and k % CHUNK_BLOCKS == 3:
                    keep_z2(c)
                keep_sums(n - 1, k - 1, sums_c, [3])
                if more:
                    take_rows_hi(n + 1, k + 1, half, False)
                if more > 1:
                    take_second(n + 2, k + 2)
                keep_h1(n, False)

            act.wait_ge(top_loaded, 7 * DMAS_IN)
            split(0, 0, 0, True)
            keep_left(0, 0, True)
            take_hi(0, 0, True)
            take_hi(0, 1, True)
            take_rows_hi(0, 0, 0, True)
            for n in range(EARLY):
                early_step(n)
            split(EARLY + 1, EARLY + 1, 0, False)
            for n in range(EARLY, CHUNK_BLOCKS + 1):
                step(n, n, (n + 1) // 2, 0, None)
            with act.Fori(1, CHUNKS - 1) as i:
                for k in range(1, CHUNK_BLOCKS + 1):
                    step(CHUNK_BLOCKS * i + k, k, 2 * i + (k + 1) // 2, i, i - 1)
            for n in range(BLOCKS - CHUNK_BLOCKS + 1, BLOCKS):
                step(n, n - (BLOCKS - CHUNK_BLOCKS), (n + 1) // 2, CHUNKS - 1, CHUNKS - 2,
                     BLOCKS - 1 - n)
            n, c = BLOCKS - 1, CHUNKS - 1
            take_h1t_hi(n)
            keep_top1(c - 1)
            for g in (0, 2):
                act.wait_ge(sums_done, GROUPS * n + g + 1)
                copy(*copy_sums_args(n, c, g, last_sums(g))).then_inc(sums_ready, 1)
            keep_top2(c - 1)
            keep_y(c - 1)
            act.wait_ge(z2_done, c + 1)
            copy(z2_sb[:], last_z2).then_inc(z2_ready, 1)
            for m in range(M1):
                act.wait_ge(top1_done, c + m + 1)
                nc.scalar.activation(top1_sb[:, m, :], last_top1(m), ACT.Relu,
                                     bias=b1_sb[:, m:m + 1]).then_inc(top1_ready, 1)
            for m in range(M2):
                act.wait_ge(top2_done, c + m + 1)
                nc.scalar.activation(top2_sb[:, m, :], last_top2(m), ACT.Relu,
                                     bias=b2_sb[:, m:m + 1]).then_inc(top2_ready, 1)
            act.wait_ge(y_done, c + 1)
            copy(y_sb[0:1, c * CHUNK:(c + 1) * CHUNK], last_y).then_inc(y_ready, 1)

        @block.tensor
        def _(pe):
            def place_left(n, k, first):
                pe.wait_ge(stack_ready, n + 1)
                if k and first:
                    pe.wait_ge(rows_lo_ready, 1)
                elif k:
                    pe.wait_ge(h1t_lo_ready, n - 1)
                s = stack[k % 2][:].rearrange("p d b -> p (d b)")
                nc.tensor.matmul(turn_ps[:], select_sb[:, 0, :], s, start=True, stop=True) \
                    .then_inc(left_done, 1)

            def place_rows(n, k):
                pe.wait_ge(left_ready, n + 1)
                for g in range(GROUPS):
                    rows = stack[k % 2][:].rearrange("p d b -> p (d b)")[:, g::GROUPS]
                    last = nc.tensor.matmul(turn_ps[:, g * SLOTS:(g + 1) * SLOTS], rows, place_sb[:],
                                            start=True, stop=True)
                last.then_inc(rows_done, 1)

            def place_right(n, k, q, first):
                if not (first and q < 2):
                    pe.wait_ge(product_ready, STEPS * n + q - 1)
                s = stack[k % 2][:].rearrange("p d b -> p (d b)")
                for a in range(tiles_of(q)):
                    last = nc.tensor.matmul(right_ps[q % 2][:, a, :],
                                            select_sb[:, 1 + 2 * q + a, :], s,
                                            start=True, stop=True)
                last.then_inc(right_done, 1)

            def layer_hi(n, q, first):
                if q == 0 and not first:
                    pe.wait_ge(h1_ready, n)
                pe.wait_ge(hi_ready, STEPS * n + q + 1)
                for t in range(2 * q, 2 * q + tiles_of(q)):
                    hi = products_hi[q][:, t % 2, :]
                    nc.tensor.matmul(h1_ps[:], w0_hi[:, t, :], hi, start=(t == 0), stop=False)
                    nc.tensor.matmul(h1_ps[:], w0_lo[:, t, :], hi, start=False, stop=False)

            def layer_lo(n, q):
                pe.wait_ge(lo_ready, STEPS * n + q + 1)
                for t in range(2 * q, 2 * q + tiles_of(q)):
                    last = nc.tensor.matmul(h1_ps[:], w0_hi[:, t, :], products_lo[q][:, t % 2, :],
                                            start=False, stop=False)
                last.then_inc(layer_done, 1)

            def layer(n, q, first):
                layer_hi(n, q, first)
                layer_lo(n, q)

            def layer_rest(n):
                pe.wait_ge(lo_ready, STEPS * (n + 1))
                nc.tensor.matmul(h1_ps[:], w0_hi[:, TILES - 1, :], products_hi[STEPS - 1][:, 0, :],
                                 start=False, stop=True).then_inc(layer_done, 1)

            def turn(n, rows):
                pe.wait_ge(h1_ready, n + 1)
                pe.wait_ge(rows_lo_ready, rows)
                for g in range(GROUPS):
                    cols = h1_sb[:].rearrange("p d b -> p (d b)")[:, g::GROUPS]
                    last = nc.tensor.transpose(turn_ps[:, g * H:(g + 1) * H], cols, ident_sb[:])
                last.then_inc(turned, 1)

            def sum_over_d(n, k, half, between):
                pe.wait_ge(h1t_lo_ready, n + 1)
                pe.wait_ge(diag_placed[k % 2], DIAG_DMAS * (half + 1))
                for g in range(GROUPS):
                    if g:
                        pe.wait_ge(sums_ready, GROUPS * n + g)
                    out_ = sums_ps[:, 0:GROUP * SLOTS]
                    hi, lo = (diag[k % 2][:, :, s, g, :] for s in range(2))
                    nc.tensor.matmul(out_, h1t_hi[:, g, :], hi, start=True, stop=False)
                    nc.tensor.matmul(out_, h1t_lo[:, g, :], hi, start=False, stop=False)
                    nc.tensor.matmul(out_, h1t_hi[:, g, :], lo, start=False, stop=True) \
                        .then_inc(sums_done, 1)
                    between(g)

            def z2(c, fields):
                if fields[0] == 0:
                    pe.wait_ge(sums_ready, GROUPS * CHUNK_BLOCKS * (c + 1))
                for f in fields:
                    last = nc.tensor.matmul(top_ps[:, 0:CHUNK], w1_sb[:, f, :], sums[:, c % 2, f, :],
                                            start=(f == 0), stop=(f == FIELDS - 1))
                if fields[-1] == FIELDS - 1:
                    last.then_inc(z2_done, 1)

            def top1(c, parts_of=range(M1)):
                pe.wait_ge(z2_ready, c + 1)
                for m in parts_of:
                    cols = slice(m * P, (m + 1) * P)
                    u = top_ps[:, m * CHUNK:(m + 1) * CHUNK]
                    nc.tensor.matmul(u, wtop1_sb[:, 0, cols], sums[:, c % 2, FIELDS, :],
                                     start=True, stop=False)
                    nc.tensor.matmul(u, wtop1_dense_sb[:, cols],
                                     dense_sb[:, bass.ds(c * CHUNK, CHUNK)],
                                     start=False, stop=False)
                    last = nc.tensor.matmul(u, wtop1_sb[:, 1, cols], z2_sb[:],
                                            start=False, stop=True)
                if parts_of[-1] == M1 - 1:
                    last.then_inc(top1_done, 1)

            def top2(c, m):
                if m == 0:
                    pe.wait_ge(top1_ready, M1 * (c + 1))
                for j in range(M1):
                    last = nc.tensor.matmul(top_ps[:, m * CHUNK:(m + 1) * CHUNK],
                                            wtop2_sb[:, j, m * P:(m + 1) * P], top1_sb[:, j, :],
                                            start=(j == 0), stop=(j == M1 - 1))
                if m == M2 - 1:
                    last.then_inc(top2_done, 1)

            def top3(c):
                pe.wait_ge(top2_ready, M2 * (c + 1))
                for m in range(M2):
                    last = nc.tensor.matmul(top_ps[0:1, 0:CHUNK], wtop3_sb[:, m:m + 1],
                                            top2_sb[:, m, :], start=(m == 0), stop=(m == M2 - 1))
                last.then_inc(y_done, 1)

            def early_step(n):
                first = n == 0
                for q in (2, 3):
                    place_right(n, n, q, first)
                for q in range(STEPS - 1):
                    layer(n, q, first)
                layer_rest(n)
                if not first:
                    turn(n - 1, n + 1)
                    sum_over_d(n - 1, n - 1, (n - 1) // 2, lambda g: None)
                place_left(n + 1, n + 1, first)
                for q in (0, 1):
                    place_right(n + 1, n + 1, q, False)
                place_rows(n + 1, n + 1)

            def step(n, k, half, c, last=False):
                phase = k % CHUNK_BLOCKS
                mlp = c is not None and phase == 0

                def some_z2(i):
                    if c is not None and phase:
                        first = (phase - 1) * Z2_CUTS[-1]
                        z2(c, range(first + Z2_CUTS[i], first + Z2_CUTS[i + 1]))

                place_right(n, k, 2, False)
                place_right(n, k, 3, False)
                if mlp:
                    top1(c, range(0, M1 // 2))
                some_z2(0)
                turn(n - 1, n + 1)
                if mlp:
                    top1(c, range(M1 // 2, M1))
                layer(n, 0, False)
                if not last:
                    place_right(n + 1, k + 1, 0, False)
                    place_left(n + 1, k + 1, False)
                    place_right(n + 1, k + 1, 1, False)

                def between(g):
                    if g == 0:
                        layer(n, 1, False)
                        if mlp:
                            top2(c, 0)
                            top2(c, 1)
                    elif g == 1:
                        layer_hi(n, 2, False)
                        some_z2(1)
                    elif g == 2:
                        layer_lo(n, 2)
                        if mlp:
                            top3(c)
                        some_z2(2)
                        if not last:
                            place_rows(n + 1, k + 1)

                sum_over_d(n - 1, k - 1, half, between)
                layer_rest(n)
                if mlp:
                    pe.wait_ge(y_ready, c + 1)

            def last_step(n, c):
                top1(c - 1, range(0, M1 // 2))
                turn(n, n + 1)
                top1(c - 1, range(M1 // 2, M1))
                pe.wait_ge(h1t_lo_ready, n + 1)
                pe.wait_ge(diag_placed[n % 2], DIAG_DMAS * (n // 2 + 1))
                for g in range(GROUPS):
                    if g == GROUPS - 1:
                        pe.wait_ge(sums_ready, GROUPS * n + 1)
                    out_ = last_sums(g)
                    hi, lo = (diag[n % 2][:, :, s, g, :] for s in range(2))
                    nc.tensor.matmul(out_, h1t_hi[:, g, :], hi, start=True, stop=False)
                    nc.tensor.matmul(out_, h1t_lo[:, g, :], hi, start=False, stop=False)
                    nc.tensor.matmul(out_, h1t_hi[:, g, :], lo, start=False, stop=True) \
                        .then_inc(sums_done, 1)
                for m in range(M2):
                    top2(c - 1, m)
                pe.wait_ge(last_sums_ready, 2)
                pe.wait_ge(sums_ready, GROUPS * n + 2)
                for m in range(M1):
                    cols = slice(m * P, (m + 1) * P)
                    nc.tensor.matmul(last_top1(m), wtop1_dense_sb[:, cols],
                                     dense_sb[:, c * CHUNK:(c + 1) * CHUNK], start=True, stop=False)
                    nc.tensor.matmul(last_top1(m), wtop1_sb[:, 0, cols], sums[:, c % 2, FIELDS, :],
                                     start=False, stop=False)
                top3(c - 1)
                for f in range(FIELDS):
                    last = nc.tensor.matmul(last_z2, w1_sb[:, f, :], sums[:, c % 2, f, :],
                                            start=(f == 0), stop=(f == FIELDS - 1))
                last.then_inc(z2_done, 1)
                pe.wait_ge(z2_ready, c + 1)
                for m in range(M1):
                    nc.tensor.matmul(last_top1(m), wtop1_sb[:, 1, m * P:(m + 1) * P], z2_sb[:],
                                     start=False, stop=True).then_inc(top1_done, 1)
                pe.wait_ge(y_ready, c)
                for j in range(M1):
                    pe.wait_ge(top1_ready, M1 * c + j + 1)
                    for m in range(M2):
                        last = nc.tensor.matmul(last_top2(m), wtop2_sb[:, j, m * P:(m + 1) * P],
                                                top1_sb[:, j, :], start=(j == 0), stop=(j == M1 - 1))
                        if j == M1 - 1:
                            last.then_inc(top2_done, 1)
                for m in range(M2):
                    pe.wait_ge(top2_ready, M2 * c + m + 1)
                    last = nc.tensor.matmul(last_y, wtop3_sb[:, m:m + 1],
                                            top2_sb[:, m, :], start=(m == 0), stop=(m == M2 - 1))
                last.then_inc(y_done, 1)

            pe.wait_ge(select_loaded, 2 * DMAS_IN)
            place_left(0, 0, True)
            place_right(0, 0, 0, True)
            place_right(0, 0, 1, True)
            place_rows(0, 0)
            pe.wait_ge(w0_step, 4)
            pe.wait_ge(ident_loaded, DMAS_IN)
            for n in range(EARLY):
                early_step(n)
            pe.wait_ge(w1_loaded, DMAS_IN)
            pe.wait_ge(top_loaded, 7 * DMAS_IN)
            for n in range(EARLY, CHUNK_BLOCKS + 1):
                step(n, n, (n - 1) // 2, None)
            with pe.Fori(1, CHUNKS - 1) as i:
                for k in range(1, CHUNK_BLOCKS + 1):
                    step(CHUNK_BLOCKS * i + k, k, 2 * i + (k - 1) // 2, i - 1)
            for n in range(BLOCKS - CHUNK_BLOCKS + 1, BLOCKS):
                step(n, n, (n - 1) // 2, CHUNKS - 2, n == BLOCKS - 1)
            last_step(BLOCKS - 1, CHUNKS - 1)


def field_of(i, j):
    f = PER_QUAD * i + j
    return f if f < FIELDS else None


def left_field(row):
    return row % FIELDS


def place_pairs():
    tiles = [{} for _ in range(TILES)]
    kinds = [range(P)[rows] for rows in (HI_HI, LO_HI, HI_LO)]
    everywhere = [f for f in range(FIELDS)
                  if all(f in [left_field(r) for r in rows] for rows in kinds)]
    left_over = everywhere[-(PAIRS - FULL_TILES * P):]
    for f in left_over:
        for rows in kinds:
            tiles[TILES - 1][next(r for r in rows if left_field(r) == f)] = f

    slots = {f: [(t, r) for t in range(FULL_TILES) for r in range(P) if left_field(r) == f]
             for f in range(FIELDS)}
    pair_at = {}

    def find_place(pair, seen):
        for f in pair:
            for slot in slots[f]:
                if slot not in pair_at:
                    pair_at[slot] = pair
                    return True
        for f in pair:
            for slot in slots[f]:
                if slot not in seen:
                    seen.add(slot)
                    if find_place(pair_at[slot], seen):
                        pair_at[slot] = pair
                        return True
        return False

    for a in range(FIELDS):
        for b in range(a, FIELDS):
            if a != b or a not in left_over:
                assert find_place((a, b), set())
    for (t, r), (a, b) in pair_at.items():
        tiles[t][r] = b if left_field(r) == a else a
    return tiles


def shape_constants(table_rows, right_fields):
    base = np.concatenate([[0], np.cumsum(table_rows)[:-1]])
    size = np.zeros((P, BLOCKS, PER_QUAD), np.int32)
    last, first_row = size.copy(), size.copy()
    select = np.zeros((P, 1 + TILES, P), np.float32)
    place = np.zeros((P, SLOTS), np.float32)
    for i in range(QUADS):
        for j in range(PER_QUAD):
            f = field_of(i, j)
            for s in range(PARTS):
                row = 32 * i + s * PER_QUAD + j
                place[row, PER_QUAD * i + j] = 1.0
                if f is None:
                    continue
                for r in range(P):
                    select[row, 0, r] = left_field(r) == f
                    for t in range(TILES):
                        select[row, 1 + t, r] = right_fields[t].get(r) == f
            if f is not None:
                quad = slice(32 * i, 32 * i + 32)
                size[quad, :, j] = table_rows[f]
                last[quad, :, j] = table_rows[f] - 1
                first_row[quad, :, j] = base[f]
    return size, last, first_row, select, place


def kernel(**inputs):
    import ml_dtypes
    import concourse.bacc as bacc
    from concourse.bass_utils import run_bass_kernel_spmd

    x = {name: np.asarray(a) for name, a in inputs.items()}
    tables = [x[f"tbl_{f}"] for f in range(FIELDS)]
    right_fields = place_pairs()
    size, last, first_row, select, place = shape_constants([t.shape[0] for t in tables], right_fields)

    ids = np.zeros((P, BLOCKS, PER_QUAD), np.int32)
    by_block = x["ids"].reshape(BLOCKS, BLOCK, FIELDS)
    for i in range(QUADS):
        for j in range(PER_QUAD):
            if field_of(i, j) is not None:
                ids[32 * i:32 * i + 32, :, j] = by_block[:, :, field_of(i, j)].T

    w0 = x["L0_rec_W0"].reshape(H, FIELDS, FIELDS)
    w0_ab = np.zeros((P, TILES, H), np.float32)
    w0_ba = np.zeros((P, TILES, H), np.float32)
    for t in range(TILES):
        for r, b in right_fields[t].items():
            a = left_field(r)
            w0_ab[r, t] = w0[:, a, b]
            if a != b:
                w0_ba[r, t] = w0[:, b, a]

    arrays = {
        "table": np.concatenate(tables, axis=0),
        "id_data": np.stack([ids, size, last, first_row], axis=1),
        "select": select.astype(ml_dtypes.bfloat16),
        "place": place.astype(ml_dtypes.bfloat16),
        "ident": np.eye(P, dtype=np.float32),
        "w0_ab": w0_ab,
        "w0_ba": w0_ba,
        "w1": x["L0_rec_W1"].reshape(H, FIELDS, H).transpose(2, 1, 0),
        "wtop1": x["W_top1"][:2 * H].reshape(2, H, TOP1).transpose(1, 0, 2),
        "wtop1_dense": x["W_top1"][2 * H:],
        "b1": x["b_top1"].reshape(M1, P).T,
        "wtop2": x["W_top2"].reshape(M1, P, TOP2).transpose(1, 0, 2),
        "b2": x["b_top2"].reshape(M2, P).T,
        "wtop3": x["W_top3"].reshape(M2, P).T,
        "dense": x["dense_ctx"].T,
    }
    arrays = {name: np.ascontiguousarray(a) for name, a in arrays.items()}
    nc = bacc.Bacc("TRN2", target_bir_lowering=False, num_devices=1)
    args = [nc.dram_tensor(name, a.shape, mybir.dt.from_np(a.dtype), kind="ExternalInput").ap()
            for name, a in arrays.items()]
    out = nc.dram_tensor("y", (1, BATCH), F32, kind="ExternalOutput").ap()
    dlrm_cin_tower(nc, *args, out)
    r = run_bass_kernel_spmd(nc, [arrays], core_ids=[0])
    return r.results[0]["y"].reshape(BATCH, 1)
```

```python
from contextlib import ExitStack

import numpy as np

import concourse.bass as bass
from concourse import mybir

F32 = mybir.dt.float32
F32R = mybir.dt.float32r
BF16 = mybir.dt.bfloat16
I32 = mybir.dt.int32
ALU = mybir.AluOpType
ACT = mybir.ActivationFunctionType

P = 128
BATCH = 512
FIELDS = 39
D = 16
H = 128
QUADS = 4
PER_QUAD = 10
SLOTS = QUADS * PER_QUAD
BLOCK = 32
BLOCKS = BATCH // BLOCK
COLS = BLOCK * D
PARTS = 3
PAIRS = FIELDS * (FIELDS + 1) // 2
OPERANDS = 5
HALVES = (((0, 2), (1, 2), (0, 1)), ((0, 4), (3, 4), (0, 3)))
PER_HALF = len(HALVES[0])
PIECES = (slice(0, 2), slice(2, 3))
TILES = 2 * PER_HALF
HI_HI, LO_HI, HI_LO = slice(0, 64), slice(64, 96), slice(96, P)
GROUP = P // D
GROUPS = BLOCK // GROUP
CHUNK_BLOCKS = 4
CHUNK = CHUNK_BLOCKS * BLOCK
CHUNKS = BATCH // CHUNK
DENSE = 16
DENSE_ROWS = 96
TOP1, TOP2 = 512, 256
M1, M2 = TOP1 // P, TOP2 // P
TOP1_HALVES = (range(0, M1 // 2), range(M1 // 2, M1))
Z2_CUTS = (0, 6, 8, FIELDS // 3)
EARLY = 1
DMAS_IN = 16


def dlrm_cin_tower(nc, table, id_data, select, place, ident, w0_ab, w0_ba,
                   w1, wtop1, wtop1_dense, b1, wtop2, b2, wtop3, dense, out):
    with ExitStack() as ctx:
        def sb(name, shape, dt):
            return ctx.enter_context(nc.sbuf_tensor(name, shape, dt))

        def psum(name, shape, dt):
            return ctx.enter_context(nc.psum_tensor(name, shape, dt))

        def sem(name):
            return ctx.enter_context(nc.semaphore(name))

        id_data_sb = sb("id_data_sb", [P, 4, BLOCKS, PER_QUAD], I32)
        rows_sb = sb("rows_sb", [P, (BLOCKS - 2 * CHUNK_BLOCKS) * PER_QUAD], I32)
        select_sb = sb("select_sb", [P, OPERANDS, P], BF16)
        place_sb = sb("place_sb", [P, SLOTS], BF16)
        ident_sb = sb("ident_sb", [P, P], F32)
        w0_ab_sb = sb("w0_ab_sb", [P, TILES + 1, H], F32)
        w0_ba_sb = sb("w0_ba_sb", [P, TILES + 1, H], F32)
        w0_sb = sb("w0_sb", [P, TILES + 1, H], F32)
        w0_hi = sb("w0_hi", [P, TILES + 1, H], F32R)
        w0_lo = sb("w0_lo", [P, TILES + 1, H], F32R)
        w1_sb = sb("w1_sb", [P, FIELDS, H], F32)
        wtop1_sb = sb("wtop1_sb", [P, 2, TOP1], F32)
        wtop1_dense_sb = sb("wtop1_dense_sb", [DENSE_ROWS, TOP1], F32)
        wtop1_dense_hl = sb("wtop1_dense_hl", [DENSE_ROWS, TOP1], F32R)
        wtop2_sb = sb("wtop2_sb", [P, M1, TOP2], F32)
        wtop3_sb = sb("wtop3_sb", [P, M2], F32)
        b1_sb = sb("b1_sb", [P, M1], F32)
        b2_sb = sb("b2_sb", [P, M2], F32)
        dense_sb = sb("dense_sb", [DENSE_ROWS, BATCH], F32)
        dense_hl = sb("dense_hl", [DENSE_ROWS, BATCH], F32R)
        y_sb = sb("y_sb", [1, BATCH], F32)

        warm = sb("warm", [1, 1], F32)
        chunk_rows = [sb(f"chunk_rows{i}", [P, CHUNK_BLOCKS * PER_QUAD], I32) for i in range(2)]
        emb = [sb(f"emb{i}", [P, PER_QUAD, D], F32) for i in range(CHUNK_BLOCKS)]
        parts = [sb(f"parts{i}", [P, D, 32], BF16) for i in range(2)]
        rest = sb("rest", [P, D, PER_QUAD], F32)
        stack = [sb(f"stack{i}", [P, D, BLOCK], BF16) for i in range(2)]
        kept = [sb(f"kept{i}", [P, 3, COLS], F32) for i in range(2)]
        products = [sb(f"products{i}", [P, PER_HALF, COLS], F32) for i in range(2)]
        products_hi = [sb(f"products_hi{i}", [P, PER_HALF, COLS], F32R) for i in range(2)]
        products_lo = [sb(f"products_lo{i}", [P, PER_HALF, COLS], F32R) for i in range(2)]
        squares = sb("squares", [P, COLS], F32)
        squares_hl = sb("squares_hl", [P, COLS], F32R)
        h1_sb = sb("h1_sb", [P, D, BLOCK], F32)
        h1t_hi = sb("h1t_hi", [P, GROUPS, H], F32R)
        h1t_lo = sb("h1t_lo", [P, GROUPS, H], F32R)
        emb_rows = [sb(f"emb_rows{i}", [P, 2, GROUPS, SLOTS], F32R) for i in range(2)]
        diag = [sb(f"diag{i}", [P, GROUP, 2, GROUPS, SLOTS], F32R) for i in range(2)]
        sums = sb("sums", [P, 2, SLOTS, CHUNK], F32)
        z2_sb = sb("z2_sb", [P, CHUNK], F32)
        top1_sb = sb("top1_sb", [P, M1, CHUNK], F32)
        top2_sb = sb("top2_sb", [P, M2, CHUNK], F32)

        outer_ps = psum("outer_ps", [P, OPERANDS - 1, COLS], F32)
        h1_ps = psum("h1_ps", [P, COLS], F32)
        turn_ps = psum("turn_ps", [P, COLS], F32)
        sums_ps = psum("sums_ps", [P, 512], F32)
        top_ps = psum("top_ps", [P, 512], F32)
        emb_rows_ps = turn_ps[:, 0:GROUPS * SLOTS]

        ids_loaded = sem("ids_loaded")
        select_loaded = sem("select_loaded")
        ident_loaded = sem("ident_loaded")
        w0_loaded = sem("w0_loaded")
        dense_loaded = sem("dense_loaded")
        w1_loaded = sem("w1_loaded")
        top_loaded = sem("top_loaded")
        gathered = [sem(f"gathered{i}") for i in range(CHUNK_BLOCKS)]
        diag_placed = [sem(f"diag_placed{i}") for i in range(2)]
        y_stored = sem("y_stored")
        ids_step = sem("ids_step")
        rows_copied = sem("rows_copied")
        zeroed = sem("zeroed")
        w0_step = sem("w0_step")
        dense_rounded = sem("dense_rounded")
        dense_split = sem("dense_split")
        first_part = sem("first_part")
        second_part = sem("second_part")
        rest_ready = sem("rest_ready")
        third_part = sem("third_part")
        stack_ready = sem("stack_ready")
        outer_ready = sem("outer_ready")
        product_ready = sem("product_ready")
        hi_ready = sem("hi_ready")
        lo_ready = sem("lo_ready")
        squares_ready = sem("squares_ready")
        squares_split = sem("squares_split")
        middle_done = sem("middle_done")
        rows_done = sem("rows_done")
        outer_done = sem("outer_done")
        layer_done = sem("layer_done")
        h1_done = sem("h1_done")
        turned = sem("turned")
        sums_done = sem("sums_done")
        z2_done = sem("z2_done")
        top1_done = sem("top1_done")
        top2_done = sem("top2_done")
        y_done = sem("y_done")
        middle_ready = sem("middle_ready")
        rows_hi_ready = sem("rows_hi_ready")
        rows_lo_ready = sem("rows_lo_ready")
        h1_ready = sem("h1_ready")
        h1t_hi_ready = sem("h1t_hi_ready")
        h1t_lo_ready = sem("h1t_lo_ready")
        sums_ready = sem("sums_ready")
        last_sums_ready = sem("last_sums_ready")
        z2_ready = sem("z2_ready")
        top1_ready = sem("top1_ready")
        top2_ready = sem("top2_ready")
        top_free = sem("top_free")

        DIAG_DMAS = GROUP * DMAS_IN
        GATHERS = PER_QUAD * DMAS_IN

        def part(k, s):
            return parts[k % 2][:, :, s * PER_QUAD:(s + 1) * PER_QUAD]

        def last_sums(g):
            return (sums_ps, h1_ps, turn_ps, sums_ps)[g][:, 0:GROUP * SLOTS]

        def last_top1(m):
            return outer_ps[:, m, 0:CHUNK]

        def last_top2(m):
            return (turn_ps, top_ps)[m][:, 0:CHUNK]

        last_z2 = h1_ps[:, 0:CHUNK]
        last_y = sums_ps[0:1, 0:CHUNK]

        def copy_sums_args(k, c, g, ps):
            at = (k % CHUNK_BLOCKS) * BLOCK + g
            return (sums[:, c % 2, :, at:at + BLOCK - GROUPS + 1:GROUPS],
                    ps.rearrange("p (b f) -> p f b", b=GROUP))

        block = ctx.enter_context(nc.Block())

        @block.sync
        def _(sp):
            sp.dma_start(id_data_sb[:], id_data).then_inc(ids_loaded, DMAS_IN)
            sp.dma_start(select_sb[:], select).then_inc(select_loaded, DMAS_IN)
            sp.dma_start(place_sb[:], place).then_inc(select_loaded, DMAS_IN)
            sp.dma_start(w0_ab_sb[:], w0_ab).then_inc(w0_loaded, DMAS_IN)
            sp.dma_start(w0_ba_sb[:], w0_ba).then_inc(w0_loaded, DMAS_IN)
            sp.dma_start(ident_sb[:], ident).then_inc(ident_loaded, DMAS_IN)
            sp.dma_start(wtop1_dense_sb[:], wtop1_dense).then_inc(dense_loaded, DMAS_IN)
            sp.dma_start(dense_sb[:], dense).then_inc(dense_loaded, DMAS_IN)
            sp.dma_start(wtop1_sb[:], wtop1).then_inc(top_loaded, DMAS_IN)
            sp.dma_start(b1_sb[:], b1).then_inc(top_loaded, DMAS_IN)
            sp.dma_start(wtop2_sb[:], wtop2).then_inc(top_loaded, DMAS_IN)
            sp.dma_start(b2_sb[:], b2).then_inc(top_loaded, DMAS_IN)
            sp.dma_start(wtop3_sb[:], wtop3).then_inc(top_loaded, DMAS_IN)
            sp.dma_start(w1_sb[:], w1).then_inc(w1_loaded, DMAS_IN)
            sp.wait_ge(zeroed, 1)

            def place_diagonal(n, k):
                sp.wait_ge(rows_lo_ready, n + 1)
                for b in range(GROUP):
                    rows = slice(b, P, GROUP)
                    sp.dma_start(diag[k % 2][rows, b].bitcast(F32),
                                 emb_rows[k % 2][rows].bitcast(F32)) \
                        .then_inc(diag_placed[k % 2], DMAS_IN)

            place_diagonal(0, 0)
            place_diagonal(1, 1)
            with sp.Fori(1, BLOCKS // 2) as i:
                for k in range(2):
                    place_diagonal(2 * i + k, k)
            sp.wait_ge(top_free, CHUNKS + 1)
            sp.dma_start(out, y_sb[0:1, :]).then_inc(y_stored, DMAS_IN)
            sp.wait_ge(y_stored, DMAS_IN)

        @block.gpsimd
        def _(pool):
            def copy_rows(c, k):
                pool.wait_ge(rest_ready, CHUNK_BLOCKS * (c - 1))
                at = bass.ds((c - 2) * CHUNK_BLOCKS * PER_QUAD, CHUNK_BLOCKS * PER_QUAD)
                nc.gpsimd.tensor_copy(chunk_rows[k][:], rows_sb[:, at]).then_inc(rows_copied, 1)
                pool.wait_ge(rows_copied, c - 1)

            def gather(n, j_chunk, k, first):
                if not first:
                    pool.wait_ge(rest_ready, n - CHUNK_BLOCKS + 1)
                for j in range(PER_QUAD):
                    rows = P if j < PER_QUAD - 1 else P - BLOCK
                    at = k * PER_QUAD + j
                    nc.gpsimd.indirect_dma_start(
                        emb[k][0:rows, j, :], None, table,
                        bass.IndirectOffsetOnAxis(ap=chunk_rows[j_chunk][0:rows, at:at + 1], axis=0),
                    ).then_inc(gathered[k], DMAS_IN)

            for c in range(2):
                pool.wait_ge(ids_step, 4 * (c + 1))
                for k in range(CHUNK_BLOCKS):
                    gather(CHUNK_BLOCKS * c + k, c, k, c == 0)
            pool.wait_ge(ids_step, 12)
            with pool.Fori(1, CHUNKS // 2) as i:
                for c in range(2):
                    copy_rows(2 * i + c, c)
                    for k in range(CHUNK_BLOCKS):
                        gather(CHUNK_BLOCKS * (2 * i + c) + k, c, k, False)

        @block.vector
        def _(dve):
            dve.wait_ge(ids_loaded, DMAS_IN)

            def number_rows(blocks, out_, steps):
                ids, size, last, base = (id_data_sb[:, i, blocks, :] for i in range(4))
                nc.vector.scalar_tensor_tensor(size, ids, 0.0, size, ALU.is_lt, ALU.mult) \
                    .then_inc(ids_step, 1)
                dve.wait_ge(ids_step, steps + 1)
                nc.vector.tensor_tensor(ids, ids, size, ALU.add).then_inc(ids_step, 1)
                dve.wait_ge(ids_step, steps + 2)
                nc.vector.tensor_tensor(ids, ids, last, ALU.min).then_inc(ids_step, 1)
                dve.wait_ge(ids_step, steps + 3)
                nc.vector.scalar_tensor_tensor(out_[:].rearrange("p (n j) -> p n j", j=PER_QUAD),
                                               ids, 0.0, base, ALU.max, ALU.add).then_inc(ids_step, 1)

            number_rows(slice(0, CHUNK_BLOCKS), chunk_rows[0], 0)
            number_rows(slice(CHUNK_BLOCKS, 2 * CHUNK_BLOCKS), chunk_rows[1], 4)
            number_rows(slice(2 * CHUNK_BLOCKS, BLOCKS), rows_sb, 8)
            for e in emb:
                nc.vector.memset(e[P - BLOCK:P, PER_QUAD - 1, :], 1.0)
            for i in range(2):
                nc.vector.memset(parts[i][:], 0.0)
            nc.vector.memset(diag[0][:].bitcast(F32), 0.0)
            nc.vector.memset(diag[1][:].bitcast(F32), 0.0).then_inc(zeroed, 1)
            dve.wait_ge(zeroed, 1)
            dve.wait_ge(w0_loaded, 2 * DMAS_IN)
            nc.vector.tensor_tensor(w0_sb[:], w0_ab_sb[:], w0_ba_sb[:], ALU.add) \
                .then_inc(w0_step, 1)
            dve.wait_ge(w0_step, 1)
            nc.vector.tensor_copy(w0_hi[:], w0_sb[:]).then_inc(w0_step, 1)
            dve.wait_ge(w0_step, 2)
            nc.vector.tensor_tensor(w0_lo[:], w0_sb[:], w0_hi[:].bitcast(F32), ALU.subtract) \
                .then_inc(w0_step, 1)
            dve.wait_ge(w0_step, 3)
            nc.vector.tensor_copy(w0_hi[LO_HI, TILES, :], w0_lo[LO_HI, TILES, :]) \
                .then_inc(w0_step, 1)

            def take_rest(n, k, first):
                dve.wait_ge(first_part, n + 1)
                if not first:
                    dve.wait_ge(third_part, n)
                nc.vector.tensor_tensor(rest[:], emb[k % CHUNK_BLOCKS][:].rearrange("p j d -> p d j"),
                                        part(k, 0), ALU.subtract).then_inc(rest_ready, 1)

            def take_third(n, k):
                dve.wait_ge(second_part, n + 1)
                nc.vector.tensor_tensor(part(k, 2), rest[:], part(k, 1), ALU.subtract) \
                    .then_inc(third_part, 1)

            def stack_parts(n, k, first):
                dve.wait_ge(third_part, n + 1)
                if not first:
                    dve.wait_ge(outer_done, 2 * (n - 1))
                nc.vector.transpose(stack[k % 2][:].rearrange("p d b -> p (d b)"),
                                    parts[k % 2][:].rearrange("p d c -> p (d c)")) \
                    .then_inc(stack_ready, 1)

            def multiply(n, k, h, first):
                dve.wait_ge(outer_ready, 2 * n + h + 1)
                if h == 0:
                    dve.wait_ge(middle_ready, n + 1)
                if not first:
                    dve.wait_ge(lo_ready, 4 * (n - 1) + 2 * h + 2)
                others = kept[k % 2][:, 0:h + 2:h + 1, :]
                second = outer_ps[:, 2 * h + 1:2 * h + 2, :].broadcast_to([P, 2, COLS])
                nc.vector.tensor_tensor(products[h][:, PIECES[0], :], second, others, ALU.mult) \
                    .then_inc(product_ready, 1)
                nc.vector.tensor_tensor(products[h][:, 2, :], others[:, 0, :], others[:, 1, :],
                                        ALU.mult).then_inc(product_ready, 1)

            def take_lo(n, h, first):
                for i, tiles in enumerate(PIECES):
                    dve.wait_ge(hi_ready, 4 * n + 2 * h + i + 1)
                    if not first:
                        dve.wait_ge(layer_done, 2 * (n - 1) + h + 1)
                    nc.vector.tensor_tensor(products_lo[h][:, tiles, :], products[h][:, tiles, :],
                                            products_hi[h][:, tiles, :].bitcast(F32),
                                            ALU.subtract).then_inc(lo_ready, 1)

            def split_squares(n):
                dve.wait_ge(squares_ready, 2 * (n + 1))
                nc.vector.tensor_tensor(squares_hl[HI_LO], squares[HI_LO],
                                        squares_hl[HI_LO].bitcast(F32), ALU.subtract) \
                    .then_inc(squares_split, 1)

            def take_rows_lo(n, k):
                dve.wait_ge(rows_hi_ready, n + 1)
                rows = [emb_rows[k % 2][:, s].rearrange("p g f -> p (g f)") for s in range(2)]
                nc.vector.tensor_tensor(rows[1], emb_rows_ps, rows[0].bitcast(F32), ALU.subtract) \
                    .then_inc(rows_lo_ready, 1)

            def take_h1t_lo(n):
                dve.wait_ge(h1t_hi_ready, n + 1)
                hi, lo = (t[:].rearrange("p g h -> p (g h)") for t in (h1t_hi, h1t_lo))
                nc.vector.tensor_tensor(lo, turn_ps[:], hi.bitcast(F32), ALU.subtract) \
                    .then_inc(h1t_lo_ready, 1)

            def split(n, k, first):
                take_rest(n, k, first)
                take_third(n, k)
                stack_parts(n, k, isinstance(n, int) and n < 2)

            def early_step(n):
                take_lo(n, 1, n == 0)
                take_rest(n + 1, n + 1, False)
                split_squares(n)
                take_third(n + 1, n + 1)
                stack_parts(n + 1, n + 1, True)
                multiply(n + 1, n + 1, 0, False)
                take_lo(n + 1, 0, False)
                take_rows_lo(n + 1, n + 1)

            def step(n, k, more=2):
                first = isinstance(n, int) and n == EARLY
                multiply(n, k, 1, False)
                if first:
                    take_rest(n + 1, k + 1, False)
                take_h1t_lo(n - 1)
                if first:
                    take_third(n + 1, k + 1)
                    stack_parts(n + 1, k + 1, False)
                take_lo(n, 1, False)
                if more:
                    multiply(n + 1, k + 1, 0, False)
                split_squares(n)
                if more:
                    take_lo(n + 1, 0, False)
                if more > 1:
                    take_rest(n + 2, k + 2, False)
                if more:
                    take_rows_lo(n + 1, k + 1)
                if more > 1:
                    take_third(n + 2, k + 2)
                    stack_parts(n + 2, k + 2, False)

            dve.wait_ge(dense_loaded, 2 * DMAS_IN)
            for all_, parts_, low in ((wtop1_dense_sb, wtop1_dense_hl, slice(64, 96)),
                                      (dense_sb, dense_hl, slice(32, 64))):
                nc.vector.tensor_copy(parts_[:], all_[:]).then_inc(dense_rounded, 1)
                dve.wait_ge(dense_rounded, 1 if all_ is wtop1_dense_sb else 2)
                nc.vector.tensor_tensor(parts_[low], all_[low], parts_[low].bitcast(F32),
                                        ALU.subtract).then_inc(dense_split, 1)

            split(0, 0, True)
            multiply(0, 0, 0, True)
            multiply(0, 0, 1, True)
            take_lo(0, 0, True)
            take_rows_lo(0, 0)
            for n in range(EARLY):
                early_step(n)
            for n in range(EARLY, CHUNK_BLOCKS + 1):
                step(n, n)
            with dve.Fori(1, CHUNKS - 1) as i:
                for k in range(1, CHUNK_BLOCKS + 1):
                    step(CHUNK_BLOCKS * i + k, k)
            for n in range(BLOCKS - CHUNK_BLOCKS + 1, BLOCKS):
                step(n, n, BLOCKS - 1 - n)
            take_h1t_lo(BLOCKS - 1)
            for g in (1, 3):
                dve.wait_ge(sums_done, GROUPS * (BLOCKS - 1) + g + 1)
                nc.vector.tensor_copy(*copy_sums_args(BLOCKS - 1, CHUNKS - 1, g, last_sums(g))) \
                    .then_inc(last_sums_ready, 1)

        @block.scalar
        def _(act):
            def copy(out_, in_):
                return nc.scalar.activation(out_, in_, ACT.Copy)

            def take_first(n, k, use, first):
                act.wait_ge(gathered[k % CHUNK_BLOCKS], GATHERS * (use + 1))
                if first:
                    act.wait_ge(zeroed, 1)
                else:
                    act.wait_ge(stack_ready, n - 1)
                copy(part(k, 0), emb[k % CHUNK_BLOCKS][:].rearrange("p j d -> p d j")) \
                    .then_inc(first_part, 1)

            def take_second(n, k):
                act.wait_ge(rest_ready, n + 1)
                copy(part(k, 1), rest[:]).then_inc(second_part, 1)

            def keep_outer(n, k, h, first):
                act.wait_ge(outer_done, 2 * n + h + 1)
                if not first:
                    act.wait_ge(product_ready, 4 * (n - 1))
                copy(kept[k % 2][:, 1 + h, :], outer_ps[:, 2 * h, :]).then_inc(outer_ready, 1)

            def take_hi(n, h, first, pieces=(0, 1)):
                for i in pieces:
                    tiles = PIECES[i]
                    act.wait_ge(product_ready, 4 * n + 2 * h + i + 1)
                    if not first:
                        act.wait_ge(layer_done, 2 * (n - 1) + h + 1)
                    copy(products_hi[h][:, tiles, :], products[h][:, tiles, :]).then_inc(hi_ready, 1)

            def square(n, k, first):
                if not first:
                    act.wait_ge(squares_split, n)
                nc.scalar.activation(squares[:], kept[k % 2][:, 0, :], ACT.Square) \
                    .then_inc(squares_ready, 1)

            def square_hi(n, k, first):
                if not first:
                    act.wait_ge(h1_done, n)
                nc.scalar.activation(squares_hl[:], kept[k % 2][:, 0, :], ACT.Square) \
                    .then_inc(squares_ready, 1)

            def keep_middle(n, k, first):
                act.wait_ge(middle_done, n + 1)
                if not first:
                    act.wait_ge(product_ready, 4 * (n - 1))
                copy(kept[k % 2][:, 0, :], turn_ps[:]).then_inc(middle_ready, 1)

            def take_rows_hi(n, k, half, first):
                act.wait_ge(rows_done, n + 1)
                if not first:
                    act.wait_ge(diag_placed[k % 2], DIAG_DMAS * half)
                copy(emb_rows[k % 2][:, 0].rearrange("p g f -> p (g f)"), emb_rows_ps) \
                    .then_inc(rows_hi_ready, 1)

            def keep_h1(n, first):
                act.wait_ge(h1_done, n + 1)
                if not first:
                    act.wait_ge(turned, n)
                copy(h1_sb[:].rearrange("p d b -> p (d b)"), h1_ps[:]).then_inc(h1_ready, 1)

            def take_h1t_hi(n):
                act.wait_ge(turned, n + 1)
                copy(h1t_hi[:].rearrange("p g h -> p (g h)"), turn_ps[:]).then_inc(h1t_hi_ready, 1)

            def keep_sums(n, k, c, groups):
                for g in groups:
                    act.wait_ge(sums_done, GROUPS * n + g + 1)
                    copy(*copy_sums_args(k, c, g, sums_ps[:, 0:GROUP * SLOTS])).then_inc(sums_ready, 1)

            def keep_z2(c):
                act.wait_ge(z2_done, c + 1)
                copy(z2_sb[:], top_ps[:, 0:CHUNK]).then_inc(z2_ready, 1)

            def keep_top1(c, half):
                act.wait_ge(top1_done, 2 * c + half + 1)
                for m in TOP1_HALVES[half]:
                    nc.scalar.activation(top1_sb[:, m, :], top_ps[:, m * CHUNK:(m + 1) * CHUNK],
                                         ACT.Relu, bias=b1_sb[:, m:m + 1]).then_inc(top1_ready, 1)

            def keep_top2(c):
                act.wait_ge(top2_done, c + 1)
                for m in range(M2):
                    nc.scalar.activation(top2_sb[:, m, :], top_ps[:, m * CHUNK:(m + 1) * CHUNK],
                                         ACT.Relu, bias=b2_sb[:, m:m + 1]).then_inc(top2_ready, 1)

            def keep_y(c):
                act.wait_ge(y_done, c + 1)
                copy(y_sb[0:1, bass.ds(c * CHUNK, CHUNK)], top_ps[0:1, 0:CHUNK]).then_inc(top_free, 1)

            def split(n, k, use, first):
                take_first(n, k, use, first)
                take_second(n, k)

            def early_step(n):
                take_hi(n, 1, n == 0)
                take_first(n + 1, n + 1, 0, n == 0)
                square(n, n, n == 0)
                square_hi(n, n, n == 0)
                take_second(n + 1, n + 1)
                keep_h1(n, n == 0)
                keep_middle(n + 1, n + 1, n == 0)
                keep_outer(n + 1, n + 1, 0, n == 0)
                take_hi(n + 1, 0, False)
                take_rows_hi(n + 1, n + 1, (n + 1) // 2, n == 0)

            def step(n, k, half, sums_c, c, more=2):
                mlp = c is not None and k % CHUNK_BLOCKS == 0
                use = sums_c + (k + 2) // CHUNK_BLOCKS
                first = isinstance(n, int) and n == EARLY
                keep_outer(n, k, 1, first)
                if first:
                    take_first(n + 1, k + 1, 0, False)
                square(n, k, False)
                take_h1t_hi(n - 1)
                if first:
                    take_second(n + 1, k + 1)
                take_hi(n, 1, False)
                if mlp:
                    keep_top1(c, 0)
                if more:
                    keep_outer(n + 1, k + 1, 0, False)
                    keep_middle(n + 1, k + 1, False)
                keep_sums(n - 1, k - 1, sums_c, [0])
                square_hi(n, k, False)
                keep_sums(n - 1, k - 1, sums_c, [1])
                if mlp:
                    keep_top1(c, 1)
                if more:
                    take_hi(n + 1, 0, False, [0])
                keep_sums(n - 1, k - 1, sums_c, [2])
                if more:
                    take_hi(n + 1, 0, False, [1])
                if more > 1:
                    take_first(n + 2, k + 2, use, False)
                if mlp:
                    keep_top2(c)
                if c is not None and k % CHUNK_BLOCKS == 3:
                    keep_z2(c)
                keep_sums(n - 1, k - 1, sums_c, [3])
                if more:
                    take_rows_hi(n + 1, k + 1, half, False)
                if more > 1:
                    take_second(n + 2, k + 2)
                keep_h1(n, False)
                if mlp:
                    keep_y(c)

            act.wait_ge(top_loaded, 5 * DMAS_IN)
            copy(warm[:], b1_sb[0:1, 0:1]).then_inc(top_free, 1)
            split(0, 0, 0, True)
            keep_middle(0, 0, True)
            keep_outer(0, 0, 0, True)
            keep_outer(0, 0, 1, True)
            take_hi(0, 0, True)
            take_rows_hi(0, 0, 0, True)
            for n in range(EARLY):
                early_step(n)
            for n in range(EARLY, CHUNK_BLOCKS + 1):
                step(n, n, (n + 1) // 2, 0, None)
            with act.Fori(1, CHUNKS - 1) as i:
                for k in range(1, CHUNK_BLOCKS + 1):
                    step(CHUNK_BLOCKS * i + k, k, 2 * i + (k + 1) // 2, i, i - 1)
            for n in range(BLOCKS - CHUNK_BLOCKS + 1, BLOCKS):
                step(n, n - (BLOCKS - CHUNK_BLOCKS), (n + 1) // 2, CHUNKS - 1, CHUNKS - 2,
                     BLOCKS - 1 - n)
            n, c = BLOCKS - 1, CHUNKS - 1
            keep_top1(c - 1, 0)
            take_h1t_hi(n)
            keep_top1(c - 1, 1)
            for g in (0, 2):
                act.wait_ge(sums_done, GROUPS * n + g + 1)
                copy(*copy_sums_args(n, c, g, last_sums(g))).then_inc(sums_ready, 1)
            keep_top2(c - 1)
            keep_y(c - 1)
            act.wait_ge(z2_done, c + 1)
            copy(z2_sb[:], last_z2).then_inc(z2_ready, 1)
            for m in range(M1):
                act.wait_ge(top1_done, 2 * c + m + 1)
                nc.scalar.activation(top1_sb[:, m, :], last_top1(m), ACT.Relu,
                                     bias=b1_sb[:, m:m + 1]).then_inc(top1_ready, 1)
            for m in range(M2):
                act.wait_ge(top2_done, c + m + 1)
                nc.scalar.activation(top2_sb[:, m, :], last_top2(m), ACT.Relu,
                                     bias=b2_sb[:, m:m + 1]).then_inc(top2_ready, 1)
            act.wait_ge(y_done, c + 1)
            copy(y_sb[0:1, c * CHUNK:(c + 1) * CHUNK], last_y).then_inc(top_free, 1)

        @block.tensor
        def _(pe):
            def place_middle(n, k, first):
                pe.wait_ge(stack_ready, n + 1)
                if k and first:
                    pe.wait_ge(rows_lo_ready, 1)
                elif k:
                    pe.wait_ge(h1t_lo_ready, n - 1)
                s = stack[k % 2][:].rearrange("p d b -> p (d b)")
                nc.tensor.matmul(turn_ps[:], select_sb[:, 0, :], s, start=True, stop=True) \
                    .then_inc(middle_done, 1)

            def place_rows(n, k):
                pe.wait_ge(middle_ready, n + 1)
                for g in range(GROUPS):
                    rows = stack[k % 2][:].rearrange("p d b -> p (d b)")[:, g::GROUPS]
                    last = nc.tensor.matmul(turn_ps[:, g * SLOTS:(g + 1) * SLOTS], rows, place_sb[:],
                                            start=True, stop=True)
                last.then_inc(rows_done, 1)

            def place_outer(n, k, h, first):
                if h == 0:
                    pe.wait_ge(stack_ready, n + 1)
                if not first:
                    pe.wait_ge(product_ready, 4 * (n - 1) + 2 * h + 2)
                s = stack[k % 2][:].rearrange("p d b -> p (d b)")
                for a in range(2 * h, 2 * h + 2):
                    last = nc.tensor.matmul(outer_ps[:, a, :], select_sb[:, 1 + a, :], s,
                                            start=True, stop=True)
                last.then_inc(outer_done, 1)

            def layer_hi(n, h, first):
                if h == 0 and not first:
                    pe.wait_ge(h1_ready, n)
                pe.wait_ge(hi_ready, 4 * n + 2 * h + 2)
                for t in range(PER_HALF):
                    hi, w = products_hi[h][:, t, :], PER_HALF * h + t
                    nc.tensor.matmul(h1_ps[:], w0_hi[:, w, :], hi, start=(w == 0), stop=False)
                    nc.tensor.matmul(h1_ps[:], w0_lo[:, w, :], hi, start=False, stop=False)

            def layer_lo(n, h):
                pe.wait_ge(lo_ready, 4 * n + 2 * h + 2)
                for t in range(PER_HALF):
                    last = nc.tensor.matmul(h1_ps[:], w0_hi[:, PER_HALF * h + t, :],
                                            products_lo[h][:, t, :], start=False, stop=False)
                last.then_inc(layer_done, 1)

            def layer_squares(n):
                pe.wait_ge(squares_split, n + 1)
                nc.tensor.matmul(h1_ps[:], w0_hi[:, TILES, :], squares_hl[:],
                                 start=False, stop=True).then_inc(h1_done, 1)

            def turn(n, rows):
                pe.wait_ge(h1_ready, n + 1)
                pe.wait_ge(rows_lo_ready, rows)
                for g in range(GROUPS):
                    cols = h1_sb[:].rearrange("p d b -> p (d b)")[:, g::GROUPS]
                    last = nc.tensor.transpose(turn_ps[:, g * H:(g + 1) * H], cols, ident_sb[:])
                last.then_inc(turned, 1)

            def sum_over_d(n, k, half, between):
                pe.wait_ge(h1t_lo_ready, n + 1)
                pe.wait_ge(diag_placed[k % 2], DIAG_DMAS * (half + 1))
                for g in range(GROUPS):
                    if g:
                        pe.wait_ge(sums_ready, GROUPS * n + g)
                    out_ = sums_ps[:, 0:GROUP * SLOTS]
                    hi, lo = (diag[k % 2][:, :, s, g, :] for s in range(2))
                    nc.tensor.matmul(out_, h1t_hi[:, g, :], hi, start=True, stop=False)
                    nc.tensor.matmul(out_, h1t_lo[:, g, :], hi, start=False, stop=False)
                    nc.tensor.matmul(out_, h1t_hi[:, g, :], lo, start=False, stop=True) \
                        .then_inc(sums_done, 1)
                    between(g)

            def z2(c, fields):
                if fields[0] == 0:
                    pe.wait_ge(sums_ready, GROUPS * CHUNK_BLOCKS * (c + 1))
                    pe.wait_ge(top_free, c + 1)
                for f in fields:
                    last = nc.tensor.matmul(top_ps[:, 0:CHUNK], w1_sb[:, f, :], sums[:, c % 2, f, :],
                                            start=(f == 0), stop=(f == FIELDS - 1))
                if fields[-1] == FIELDS - 1:
                    last.then_inc(z2_done, 1)

            def top1(c, half):
                if half == 0:
                    pe.wait_ge(z2_ready, c + 1)
                else:
                    pe.wait_ge(top1_ready, M1 * c + len(TOP1_HALVES[0]))
                for m in TOP1_HALVES[half]:
                    cols = slice(m * P, (m + 1) * P)
                    u = top_ps[:, m * CHUNK:(m + 1) * CHUNK]
                    nc.tensor.matmul(u, wtop1_sb[:, 0, cols], sums[:, c % 2, FIELDS, :],
                                     start=True, stop=False)
                    nc.tensor.matmul(u, wtop1_dense_hl[:, cols],
                                     dense_hl[:, bass.ds(c * CHUNK, CHUNK)],
                                     start=False, stop=False)
                    last = nc.tensor.matmul(u, wtop1_sb[:, 1, cols], z2_sb[:],
                                            start=False, stop=True)
                last.then_inc(top1_done, 1)

            def top2(c, m):
                if m == 0:
                    pe.wait_ge(top1_ready, M1 * (c + 1))
                for j in range(M1):
                    last = nc.tensor.matmul(top_ps[:, m * CHUNK:(m + 1) * CHUNK],
                                            wtop2_sb[:, j, m * P:(m + 1) * P], top1_sb[:, j, :],
                                            start=(j == 0), stop=(j == M1 - 1))
                if m == M2 - 1:
                    last.then_inc(top2_done, 1)

            def top3(c):
                pe.wait_ge(top2_ready, M2 * (c + 1))
                for m in range(M2):
                    last = nc.tensor.matmul(top_ps[0:1, 0:CHUNK], wtop3_sb[:, m:m + 1],
                                            top2_sb[:, m, :], start=(m == 0), stop=(m == M2 - 1))
                last.then_inc(y_done, 1)

            def early_step(n):
                first = n == 0
                for h in range(2):
                    layer_hi(n, h, first)
                    layer_lo(n, h)
                layer_squares(n)
                place_middle(n + 1, n + 1, first)
                place_outer(n + 1, n + 1, 0, False)
                place_rows(n + 1, n + 1)

            def step(n, k, half, c, last=False):
                phase = k % CHUNK_BLOCKS
                mlp = c is not None and phase == 0

                def some_z2(i):
                    if c is not None and phase:
                        first = (phase - 1) * Z2_CUTS[-1]
                        z2(c, range(first + Z2_CUTS[i], first + Z2_CUTS[i + 1]))

                place_outer(n, k, 1, False)
                if mlp:
                    top1(c, 0)
                some_z2(0)
                turn(n - 1, n + 1)
                first = isinstance(n, int) and n == EARLY
                if not last and not first:
                    place_outer(n + 1, k + 1, 0, False)
                layer_hi(n, 0, False)
                layer_lo(n, 0)
                if first:
                    place_outer(n + 1, k + 1, 0, False)
                if not last:
                    place_middle(n + 1, k + 1, False)

                def between(g):
                    if g == 0:
                        layer_hi(n, 1, False)
                        if mlp:
                            top1(c, 1)
                    elif g == 1:
                        layer_lo(n, 1)
                        some_z2(1)
                    elif g == 2:
                        if not last:
                            place_rows(n + 1, k + 1)
                        if mlp:
                            for m in range(M2):
                                top2(c, m)
                        some_z2(2)

                sum_over_d(n - 1, k - 1, half, between)
                layer_squares(n)
                if mlp:
                    top3(c)

            def last_step(n, c):
                top1(c - 1, 0)
                turn(n, n + 1)
                pe.wait_ge(product_ready, 4 * (n + 1))
                for m in range(M1):
                    nc.tensor.matmul(last_top1(m), wtop1_dense_hl[:, m * P:(m + 1) * P],
                                     dense_hl[:, c * CHUNK:(c + 1) * CHUNK], start=True, stop=False)
                top1(c - 1, 1)
                pe.wait_ge(h1t_lo_ready, n + 1)
                pe.wait_ge(diag_placed[n % 2], DIAG_DMAS * (n // 2 + 1))
                for g in range(GROUPS):
                    if g == GROUPS - 1:
                        pe.wait_ge(sums_ready, GROUPS * n + 1)
                    out_ = last_sums(g)
                    hi, lo = (diag[n % 2][:, :, s, g, :] for s in range(2))
                    nc.tensor.matmul(out_, h1t_hi[:, g, :], hi, start=True, stop=False)
                    nc.tensor.matmul(out_, h1t_lo[:, g, :], hi, start=False, stop=False)
                    nc.tensor.matmul(out_, h1t_hi[:, g, :], lo, start=False, stop=True) \
                        .then_inc(sums_done, 1)
                for m in range(M2):
                    top2(c - 1, m)
                pe.wait_ge(last_sums_ready, 2)
                pe.wait_ge(sums_ready, GROUPS * n + 2)
                for m in range(M1):
                    nc.tensor.matmul(last_top1(m), wtop1_sb[:, 0, m * P:(m + 1) * P],
                                     sums[:, c % 2, FIELDS, :], start=False, stop=False)
                top3(c - 1)
                for f in range(FIELDS):
                    last = nc.tensor.matmul(last_z2, w1_sb[:, f, :], sums[:, c % 2, f, :],
                                            start=(f == 0), stop=(f == FIELDS - 1))
                last.then_inc(z2_done, 1)
                pe.wait_ge(z2_ready, c + 1)
                for m in range(M1):
                    nc.tensor.matmul(last_top1(m), wtop1_sb[:, 1, m * P:(m + 1) * P], z2_sb[:],
                                     start=False, stop=True).then_inc(top1_done, 1)
                pe.wait_ge(top_free, c + 1)
                for j in range(M1):
                    pe.wait_ge(top1_ready, M1 * c + j + 1)
                    for m in range(M2):
                        last = nc.tensor.matmul(last_top2(m), wtop2_sb[:, j, m * P:(m + 1) * P],
                                                top1_sb[:, j, :], start=(j == 0), stop=(j == M1 - 1))
                        if j == M1 - 1:
                            last.then_inc(top2_done, 1)
                for m in range(M2):
                    pe.wait_ge(top2_ready, M2 * c + m + 1)
                    last = nc.tensor.matmul(last_y, wtop3_sb[:, m:m + 1],
                                            top2_sb[:, m, :], start=(m == 0), stop=(m == M2 - 1))
                last.then_inc(y_done, 1)

            def keep_warm(count):
                for _ in range(count):
                    nc.tensor.matmul(top_ps[:], select_sb[:, 0, :],
                                     select_sb[:].rearrange("p a r -> p (a r)")[:, 0:COLS],
                                     start=True, stop=True)

            pe.wait_ge(select_loaded, 2 * DMAS_IN)
            pe.wait_ge(dense_split, 2)
            keep_warm(10)
            place_middle(0, 0, True)
            place_outer(0, 0, 0, True)
            place_outer(0, 0, 1, True)
            place_rows(0, 0)
            keep_warm(6)
            pe.wait_ge(w0_step, 4)
            pe.wait_ge(ident_loaded, DMAS_IN)
            for n in range(EARLY):
                early_step(n)
            keep_warm(16)
            pe.wait_ge(w1_loaded, DMAS_IN)
            pe.wait_ge(top_loaded, 5 * DMAS_IN)
            pe.wait_ge(dense_split, 2)
            for n in range(EARLY, CHUNK_BLOCKS + 1):
                step(n, n, (n - 1) // 2, None)
            with pe.Fori(1, CHUNKS - 1) as i:
                for k in range(1, CHUNK_BLOCKS + 1):
                    step(CHUNK_BLOCKS * i + k, k, 2 * i + (k - 1) // 2, i - 1)
            for n in range(BLOCKS - CHUNK_BLOCKS + 1, BLOCKS):
                step(n, n, (n - 1) // 2, CHUNKS - 2, n == BLOCKS - 1)
            last_step(BLOCKS - 1, CHUNKS - 1)


def field_of(i, j):
    f = PER_QUAD * i + j
    return f if f < FIELDS else None


def bowties():
    third = FIELDS // 3

    def field(x, level):
        return third * (level % 3) + x % third

    triples = {f: [] for f in range(FIELDS)}
    for x in range(third):
        for level in range(3):
            for y in range(x + 1, third):
                z = (x + y) * (third + 1) // 2
                triples[field(z, level + 1)].append({field(x, level), field(y, level),
                                                     field(z, level + 1)})
        triples[field(x, x % 2)].append({field(x, level) for level in range(3)})

    while sum(-(-len(t) // 2) for t in triples.values()) > P:
        f, triple, g = next((f, triple, g) for f in triples if len(triples[f]) % 2
                            for triple in triples[f]
                            for g in triple if g != f and len(triples[g]) % 2)
        triples[f].remove(triple)
        triples[g].append(triple)

    rows = []
    for f in triples:
        for i in range(0, len(triples[f]), 2):
            outer = [sorted(t - {f}) for t in triples[f][i:i + 2]] + [[f, f]]
            rows.append((f, *outer[0], *outer[1]))
    return rows


def place_bowties():
    kinds = [list(range(P)[rows]) for rows in (HI_HI, LO_HI, HI_LO)]
    rows = bowties()
    squared = {row[0] for row in rows if row[0] in row[1:]}
    placed, squares = {}, {}
    for f in range(FIELDS):
        if f not in squared:
            for kind, row in zip(kinds, [row for row in rows if row[0] == f]):
                at = kind.pop(0)
                placed[at], squares[at] = row, f
                rows.remove(row)
    free = [at for kind in kinds for at in kind]
    placed.update(zip(free, rows))
    return [placed[at] for at in range(P)], squares


def shape_constants(table_rows, operands):
    base = np.concatenate([[0], np.cumsum(table_rows)[:-1]])
    size = np.zeros((P, BLOCKS, PER_QUAD), np.int32)
    last, first_row = size.copy(), size.copy()
    select = np.zeros((P, OPERANDS, P), np.float32)
    place = np.zeros((P, SLOTS), np.float32)
    for i in range(QUADS):
        for j in range(PER_QUAD):
            f = field_of(i, j)
            for s in range(PARTS):
                row = 32 * i + s * PER_QUAD + j
                place[row, PER_QUAD * i + j] = 1.0
                if f is None:
                    continue
                for r in range(P):
                    for a in range(OPERANDS):
                        select[row, a, r] = operands[r][a] == f
            if f is not None:
                quad = slice(32 * i, 32 * i + 32)
                size[quad, :, j] = table_rows[f]
                last[quad, :, j] = table_rows[f] - 1
                first_row[quad, :, j] = base[f]
    return size, last, first_row, select, place


def three_times(a):
    out = np.zeros((DENSE_ROWS, a.shape[1]), np.float32)
    for start in range(0, DENSE_ROWS, 32):
        out[start:start + DENSE] = a
    return out


def kernel(**inputs):
    import ml_dtypes
    import concourse.bacc as bacc
    from concourse.bass_utils import run_bass_kernel_spmd

    x = {name: np.asarray(a) for name, a in inputs.items()}
    tables = [x[f"tbl_{f}"] for f in range(FIELDS)]
    operands, squares = place_bowties()
    size, last, first_row, select, place = shape_constants([t.shape[0] for t in tables], operands)

    ids = np.zeros((P, BLOCKS, PER_QUAD), np.int32)
    by_block = x["ids"].reshape(BLOCKS, BLOCK, FIELDS)
    for i in range(QUADS):
        for j in range(PER_QUAD):
            if field_of(i, j) is not None:
                ids[32 * i:32 * i + 32, :, j] = by_block[:, :, field_of(i, j)].T

    w0 = x["L0_rec_W0"].reshape(H, FIELDS, FIELDS)
    w0_ab = np.zeros((P, TILES + 1, H), np.float32)
    w0_ba = np.zeros((P, TILES + 1, H), np.float32)
    done = {(f, f) for f in squares.values()}
    for t, (i, j) in enumerate(HALVES[0] + HALVES[1]):
        for r in range(P):
            a, b = sorted((operands[r][i], operands[r][j]))
            if (a, b) not in done:
                done.add((a, b))
                w0_ab[r, t] = w0[:, a, b]
                if a != b:
                    w0_ba[r, t] = w0[:, b, a]
    assert len(done) == PAIRS
    for r, f in squares.items():
        w0_ab[r, TILES] = w0[:, f, f]

    arrays = {
        "table": np.concatenate(tables, axis=0),
        "id_data": np.stack([ids, size, last, first_row], axis=1),
        "select": select.astype(ml_dtypes.bfloat16),
        "place": place.astype(ml_dtypes.bfloat16),
        "ident": np.eye(P, dtype=np.float32),
        "w0_ab": w0_ab,
        "w0_ba": w0_ba,
        "w1": x["L0_rec_W1"].reshape(H, FIELDS, H).transpose(2, 1, 0),
        "wtop1": x["W_top1"][:2 * H].reshape(2, H, TOP1).transpose(1, 0, 2),
        "wtop1_dense": three_times(x["W_top1"][2 * H:]),
        "b1": x["b_top1"].reshape(M1, P).T,
        "wtop2": x["W_top2"].reshape(M1, P, TOP2).transpose(1, 0, 2),
        "b2": x["b_top2"].reshape(M2, P).T,
        "wtop3": x["W_top3"].reshape(M2, P).T,
        "dense": three_times(x["dense_ctx"].T),
    }
    arrays = {name: np.ascontiguousarray(a) for name, a in arrays.items()}
    nc = bacc.Bacc("TRN2", target_bir_lowering=False, num_devices=1)
    args = [nc.dram_tensor(name, a.shape, mybir.dt.from_np(a.dtype), kind="ExternalInput").ap()
            for name, a in arrays.items()]
    out = nc.dram_tensor("y", (1, BATCH), F32, kind="ExternalOutput").ap()
    dlrm_cin_tower(nc, *args, out)
    r = run_bass_kernel_spmd(nc, [arrays], core_ids=[0])
    return r.results[0]["y"].reshape(BATCH, 1)
```
